# Optimizing a Trainium2 kernel written in Bass

```python
import numpy as np
import jax
import jax.numpy as jnp

def _softmax(x, axis=-1):
    return jax.nn.softmax(x, axis=axis)

def _gelu(x):
    return jax.nn.gelu(x, approximate=True)

def _silu(x):
    return jax.nn.silu(x)

def _sigmoid(x):
    return jax.nn.sigmoid(x)

def _layernorm(x, axis=-1, eps=1e-05):
    m = jnp.mean(x, axis=axis, keepdims=True)
    v = jnp.var(x, axis=axis, keepdims=True)
    return (x - m) / jnp.sqrt(v + eps)

def _scatter_add(tgt, idx, src, axis=0):
    return tgt.at[idx].add(src)

def _segment_sum(src, seg, n):
    return jax.ops.segment_sum(src, seg, n)
kernel_name = 'mk_xattn_ffn_d1_seqx_r8_c1285b'

def setup_inputs(seed: int=0):
    np.random.seed(seed)
    _w = jnp.asarray

    def _rec_inputs():
        import jax
        import jax.numpy as jnp
        _rk = jax.random.key(seed)
        x = -0.0002928 + 1 * jax.random.normal(jax.random.fold_in(_rk, 1), (32, 100, 128), jnp.float32)
        _lenS = 100 - jax.random.randint(jax.random.fold_in(_rk, 7), (32,), 0, max(1, 100 // 4) + 1, jnp.int32)
        _lenS2 = 1444 - jax.random.randint(jax.random.fold_in(_rk, 8), (32,), 0, max(1, 1444 // 4) + 1, jnp.int32)
        _ctx_1024P = jax.random.normal(jax.random.fold_in(_rk, 11), (32, 16, 128), jnp.float32)
        _ctx_1024c = jax.random.dirichlet(jax.random.fold_in(_rk, 511), 0.3 * jnp.ones((16,), jnp.float32), (32, 1444))
        _ctx_1024t = jnp.einsum('bsk,bkd->bsd', _ctx_1024c, _ctx_1024P)
        _ctx_1024t = _ctx_1024t * jax.lax.rsqrt(jnp.mean(jnp.square(_ctx_1024t)) + 1e-12) * 0.953939
        ctx_1024 = -1.39393e-06 + 0.999914 * (_ctx_1024t + 0.3 * jax.random.normal(jax.random.fold_in(_rk, 611), (32, 1444, 128), jnp.float32))
        _validS = jnp.arange(100)[None, :] < _lenS[:, None]
        _validS2 = jnp.arange(1444)[None, :] < _lenS2[:, None]
        _causal = jnp.tril(jnp.ones((100, 100), dtype=bool))
        mask_BxS_bf1 = jnp.ones((32, 100), dtype=bool)
        return (x, ctx_1024, mask_BxS_bf1)
    x, ctx_1024, mask_BxS_bf1 = _rec_inputs()

    def _L0_xattn_setup():
        import jax, jax.numpy as jnp
        import numpy as np
        NUM_HEADS = 16
        TOKEN_DIM = 128
        D_HEAD = TOKEN_DIM // NUM_HEADS

        def masked_softmax(scores, mask):
            scores = jnp.clip(scores, -50.0, 50.0)
            exp_scores = jnp.exp(scores)
            if mask is not None:
                exp_scores = jnp.where(mask, exp_scores, 0.0)
            denom = jnp.sum(exp_scores, axis=-1, keepdims=True)
            denom = jnp.where(denom <= 0.0, 1.0, denom)
            return exp_scores / denom
        key = jax.random.key(seed)
        ks = jax.random.split(key, 8)
        B, Sq, Sk = (2, 256, 256)
        scale = 1.0 / np.sqrt(TOKEN_DIM)
        return {'Q': jax.random.normal(ks[0], (B, Sq, TOKEN_DIM), dtype=jnp.float32), 'K': jax.random.normal(ks[1], (B, Sk, TOKEN_DIM), dtype=jnp.float32), 'V': jax.random.normal(ks[2], (B, Sk, TOKEN_DIM), dtype=jnp.float32), 'mask': jnp.ones((B, Sq), dtype=bool), 'W_q': jax.random.normal(ks[3], (TOKEN_DIM, TOKEN_DIM), dtype=jnp.float32) * scale, 'W_k': jax.random.normal(ks[4], (TOKEN_DIM, TOKEN_DIM), dtype=jnp.float32) * scale, 'W_v': jax.random.normal(ks[5], (TOKEN_DIM, TOKEN_DIM), dtype=jnp.float32) * scale, 'W_o': jax.random.normal(ks[6], (TOKEN_DIM, TOKEN_DIM), dtype=jnp.float32) * scale}
    _L0_xattn_all = _L0_xattn_setup()
    _L0_xattn_in = {k: v for k, v in _L0_xattn_all.items() if k in ('W_q', 'W_k', 'W_v', 'W_o')}
    del _L0_xattn_all

    def _L0_ffn_setup():
        import jax, jax.numpy as jnp
        import numpy as np
        TOP_K = 2
        key = jax.random.key(seed)
        k1, k2, k3, k4 = jax.random.split(key, 4)
        B, N, D, E, F = (4, 256, 128, 8, 512)
        x = jax.random.normal(k1, (B, N, D), dtype=jnp.float32)
        gate_w = jax.random.normal(k2, (D, E), dtype=jnp.float32) * D ** (-0.5)
        w1 = jax.random.normal(k3, (E, D, F), dtype=jnp.float32) * D ** (-0.5)
        w2 = jax.random.normal(k4, (E, F, D), dtype=jnp.float32) * F ** (-0.5)
        return {'x': x, 'gate_w': gate_w, 'w1': w1, 'w2': w2}
    _L0_ffn_all = _L0_ffn_setup()
    _L0_ffn_in = {k: v for k, v in _L0_ffn_all.items() if k in ('gate_w', 'w1', 'w2')}
    del _L0_ffn_all
    return {'x': x, 'ctx_1024': ctx_1024, 'mask_BxS_bf1': mask_BxS_bf1, 'L0_xattn_W_q': _L0_xattn_in['W_q'], 'L0_xattn_W_k': _L0_xattn_in['W_k'], 'L0_xattn_W_v': _L0_xattn_in['W_v'], 'L0_xattn_W_o': _L0_xattn_in['W_o'], 'L0_ffn_gate_w': _L0_ffn_in['gate_w'], 'L0_ffn_w1': _L0_ffn_in['w1'], 'L0_ffn_w2': _L0_ffn_in['w2']}

def reference(x, ctx_1024, mask_BxS_bf1, L0_xattn_W_q, L0_xattn_W_k, L0_xattn_W_v, L0_xattn_W_o, L0_ffn_gate_w, L0_ffn_w1, L0_ffn_w2):
    import jax
    import jax.numpy as jnp

    def _L0_xattn_ref(Q, K, V, mask, W_q, W_k, W_v, W_o):
        import jax, jax.numpy as jnp
        import numpy as np
        NUM_HEADS = 16
        TOKEN_DIM = 128
        D_HEAD = TOKEN_DIM // NUM_HEADS

        def masked_softmax(scores, mask):
            scores = jnp.clip(scores, -50.0, 50.0)
            exp_scores = jnp.exp(scores)
            if mask is not None:
                exp_scores = jnp.where(mask, exp_scores, 0.0)
            denom = jnp.sum(exp_scores, axis=-1, keepdims=True)
            denom = jnp.where(denom <= 0.0, 1.0, denom)
            return exp_scores / denom
        B = Q.shape[0]
        q = (Q @ W_q.T).reshape(B, -1, NUM_HEADS, D_HEAD).transpose(0, 2, 1, 3)
        k = (K @ W_k.T).reshape(B, -1, NUM_HEADS, D_HEAD).transpose(0, 2, 1, 3)
        v = (V @ W_v.T).reshape(B, -1, NUM_HEADS, D_HEAD).transpose(0, 2, 1, 3)
        scores = jnp.einsum('bhqd,bhkd->bhqk', q, k) / np.sqrt(D_HEAD)
        m = mask[:, None, :, None] if mask is not None else None
        attn = masked_softmax(scores, m)
        out = jnp.einsum('bhqk,bhkd->bhqd', attn, v)
        out = out.transpose(0, 2, 1, 3).reshape(B, -1, NUM_HEADS * D_HEAD)
        return out @ W_o.T

    def _L0_ffn_ref(x, gate_w, w1, w2):
        import jax, jax.numpy as jnp
        import numpy as np
        TOP_K = 2
        E = gate_w.shape[-1]
        gate_logits = jnp.einsum('bnd,de->bne', x, gate_w)
        gate_probs = jax.nn.softmax(gate_logits, axis=-1)
        top_k_probs, top_k_idx = jax.lax.top_k(gate_probs, TOP_K)
        top_k_weights = top_k_probs / jnp.sum(top_k_probs, axis=-1, keepdims=True)
        comb = jnp.sum(jax.nn.one_hot(top_k_idx, E, dtype=x.dtype) * top_k_weights[..., None], axis=2)
        h = jax.nn.gelu(jnp.einsum('bnd,edf->benf', x, w1))
        expert_out = jnp.einsum('benf,efd->bend', h, w2)
        output = jnp.einsum('bne,bend->bnd', comb, expert_out)
        return output
    x = x + _L0_xattn_ref(_layernorm(x, axis=-1), ctx_1024, ctx_1024, mask_BxS_bf1, L0_xattn_W_q, L0_xattn_W_k, L0_xattn_W_v, L0_xattn_W_o)
    x = x + _L0_ffn_ref(_layernorm(x, axis=-1), L0_ffn_gate_w, L0_ffn_w1, L0_ffn_w2)
    return x

_drawn_inputs = setup_inputs


def setup_inputs(seed=0):
    import zlib

    import numpy as np

    out = dict(_drawn_inputs(seed))
    spreads = {}
    factors = {}
    for name, (base, spread) in spreads.items():
        noise = np.random.default_rng([zlib.crc32(name.encode()), seed]).standard_normal(out[name].shape)
        drawn = base * np.exp(spread * noise) if base else spread * noise
        out[name] = jnp.asarray(drawn.astype(out[name].dtype))
    for name, factor in factors.items():
        out[name] = (out[name] * factor).astype(out[name].dtype)
    return out
```

```python
from contextlib import ExitStack
import math

import numpy as np
import concourse.bass as bass
from concourse import mybir

F32 = mybir.dt.float32
F32R = mybir.dt.float32r
U8 = mybir.dt.uint8
U32 = mybir.dt.uint32
ALU = mybir.AluOpType
ACT = mybir.ActivationFunctionType
AX = mybir.AxisListType

P = 128
HEADS = 16
EPS = 1e-5
CLIP = 50.0
TOP = 2


def xattn_moe(nc, x, ctx, mask, W_q, W_k, W_v, W_o, gate_w, w1, w2, out):
    B, SQ, D = x.shape
    SK = ctx.shape[1]
    E, _, F = w1.shape
    DH = D // HEADS
    TILES = -(-SK // P)
    FULL = SK // P
    TAIL = SK - FULL * P
    GROUPS = 4
    HG = HEADS // GROUPS
    GQ = HG * SQ
    PAIRS = HEADS // 2
    VW = 2 * DH + 1
    PQ = 2 * SQ
    CB = 3
    CHUNKS = TILES * GROUPS // CB
    RING = 4
    KC = 4
    KSTEPS = TILES // KC
    SCALE = 1.0 / math.sqrt(DH)
    LOW, HIGH = float(np.exp(np.float32(-CLIP))), float(np.exp(np.float32(CLIP)))
    KD = 16 * 4 * GROUPS
    QB = 4
    NQ = QB * SQ
    QSTEPS = B // QB
    FC = F // P
    assert CHUNKS == 16 and TILES == 12 and B % 2 == 0 and D == P

    QUERIES, VALUES = 2 * KSTEPS, 2 * KSTEPS + 1
    PREP, FINISH = 3 * KSTEPS + 1, 3

    def scratch_base(b):
        if isinstance(b, int) and b == 0:
            return PREP
        return (PREP + FINISH) * b + (PREP - FINISH)

    es = ExitStack()
    with es:
        def sb(name, shape, dt=F32):
            return es.enter_context(nc.sbuf_tensor(name, shape, dt))

        def ps(name, shape):
            return es.enter_context(nc.psum_tensor(name, shape, F32))

        def sem(name):
            return es.enter_context(nc.semaphore(name))

        ident = sb("ident", [P, P])
        x_all = sb("x_all", [SQ, B, D])
        normed = sb("normed", [SQ, 2, QB, D])
        stats = sb("stats", [SQ, B, 6])
        moments = sb("moments", [SQ, B, 2])
        var_eps = sb("var_eps", [SQ, B])
        std = sb("std", [SQ, B])
        rstd0 = sb("rstd0", [SQ, B])
        newton = sb("newton", [SQ, B])
        rstd = sb("rstd", [SQ, B])
        mask_u8 = sb("mask_u8", [B, SQ], U8)
        mask_rows = sb("mask_rows", [B, SQ])
        mask_f = sb("mask_f", [SQ, B])
        w_nat = sb("w_nat", [P, 4, P])
        w_turned = sb("w_turned", [P, 4, P])
        wq_rep = sb("wq_rep", [P, GROUPS, 4, HG * DH])
        xT = sb("xT", [P, B * SQ])
        q_parts = sb("q_parts", [P, GROUPS, SQ], F32R)
        own_head = sb("own_head", [P, 4, HG])
        head_mask = sb("head_mask", [P, HG])
        q_stack = [sb(f"q_stack{p}", [P, GROUPS, HG, SQ], F32R) for p in range(2)]
        ctx_nat = [sb(f"ctx_nat{p}", [P, TILES, D]) for p in range(2)]
        ctxT = sb("ctxT", [P, TILES * P])
        k_full = sb("k_full", [P, KSTEPS, KC * P])
        q_full = sb("q_full", [P, GROUPS * SQ])
        k_hi = sb("k_hi", [P, TILES * P], F32R)
        k_lo = sb("k_lo", [P, TILES * P], F32R)
        k_stack = [sb(f"k_stack{p}", [P, GROUPS, TILES * P], F32R) for p in range(2)]
        v_both = sb("v_both", [P, 2, TILES, PAIRS, VW])
        v_ones = [v_both[:, p, :, :, :] for p in range(2)]
        probs = sb("probs", [P, RING, CB, GQ])
        o_raw = sb("o_raw", [P, GQ])
        rden = sb("rden", [SQ, 4, GROUPS])
        attn = sb("attn", [SQ, D])
        attnT = sb("attnT", [P, SQ])

        scores = ps("scores", [P, 2, CB, 512])
        o_sum = ps("o_sum", [P, 512])
        scratch = ps("scratch", [P, 512])

        x_loaded = sem("x_loaded")
        w_loaded = sem("w_loaded")
        mask_loaded = sem("mask_loaded")
        mask_cast = sem("mask_cast")
        mask_in_psum = sem("mask_in_psum")
        mask_ready = sem("mask_ready")
        gate_diff = sem("gate_diff")
        cleared = sem("cleared")
        ident_ready = sem("ident_ready")
        o_cleared = sem("o_cleared")
        stats_ready = sem("stats_ready")
        rstd_step = sem("rstd_step")
        std_ready = sem("std_ready")
        normed_ready = sem("normed_ready")
        w_in_psum = sem("w_in_psum")
        w_turned_ready = sem("w_turned_ready")
        xT_in_psum = sem("xT_in_psum")
        xT_ready = sem("xT_ready")
        wq_rep_ready = sem("wq_rep_ready")
        own_head_step = sem("own_head_step")
        head_mask_ready = sem("head_mask_ready")
        q_hi_ready = sem("q_hi_ready")
        q_stacked = sem("q_stacked")
        ctx_loaded = [sem(f"ctx_loaded{p}") for p in range(2)]
        scratch_filled = sem("scratch_filled")
        scratch_emptied = sem("scratch_emptied")
        k_hi_ready = sem("k_hi_ready")
        k_split = sem("k_split")
        q_split = sem("q_split")
        k_stacked = sem("k_stacked")
        scores_ready = sem("scores_ready")
        exp_ready = sem("exp_ready")
        probs_ready = sem("probs_ready")
        pv_done = sem("pv_done")
        o_taken = sem("o_taken")
        rden_ready = sem("rden_ready")
        x1_ready = sem("x1_ready")
        moments_ready = sem("moments_ready")
        std2_ready = sem("std2_ready")
        rstd2_step = sem("rstd2_step")
        normed2_ready = sem("normed2_ready")
        experts_loaded = sem("experts_loaded")
        zT_in_psum = sem("zT_in_psum")
        zT_ready = sem("zT_ready")
        logits_in_psum = sem("logits_in_psum")
        logits_ready = sem("logits_ready")
        gate_step = sem("gate_step")
        gate_exp = sem("gate_exp")
        comb_ready = sem("comb_ready")
        h_in_psum = sem("h_in_psum")
        h_ready = sem("h_ready")
        y_in_psum = sem("y_in_psum")
        y_added = sem("y_added")
        out_stored = sem("out_stored")
        iota_ready = sem("iota_ready")

        WQ, WK, WV, WO = range(4)

        w1_sb = sb("w1_sb", [P, E, F])
        gate_sb = sb("gate_sb", [P, E])
        small = w_nat[:].rearrange("p n d -> p (n d)")[0:SQ, 0:5 * QB * E].rearrange(
            "q (n b e) -> q n b e", n=5, b=QB)
        logits = small[:, 0, :, :]
        top8 = small[:, 1, :, :]
        top_at = sb("top_at", [SQ, QB, E], U32)
        top_atf = small[:, 2, :, :]
        eids = sb("eids", [SQ, E])
        eids_i = sb("eids_i", [SQ, E], mybir.dt.int32)
        neg_max = sb("neg_max", [SQ, QB])
        e2 = sb("e2", [SQ, QB])
        wsum = sb("wsum", [SQ, QB])
        wt = sb("wt", [SQ, QB, 2])
        pick = small[:, 3, :, :]
        comb = small[:, 4, :, :]

        h_sb = v_both[:].rearrange("p a t n w -> p (a t n w)")[:, 0:8 * NQ].rearrange(
            "p (n c q) -> p n c q", n=4, c=2)
        w2_sb = probs[:].rearrange("p r m q -> p (r m q)")[:, 0:E * FC * D].rearrange(
            "p (e c d) -> p e c d", e=E, c=FC)

        block = es.enter_context(nc.Block())

        @block.sync
        def _(sp):
            sp.dma_start(x_all[:], x.rearrange("b q d -> q b d")).then_inc(x_loaded, 16)
            for n, w in enumerate((W_q, W_k, W_v, W_o)):
                sp.dma_start(w_nat[:, n, :], w).then_inc(w_loaded, 16)
            sp.dma_start(mask_u8[:], mask).then_inc(mask_loaded, 16)

            def load_ctx(b, p):
                sp.dma_start(ctx_nat[p][:, 0:FULL, :],
                             ctx[b, 0:FULL * P, :].rearrange("(p t) d -> p t d", t=FULL)
                             ).then_inc(ctx_loaded[p], 16)
                sp.dma_start(ctx_nat[p][0:TAIL, FULL, :], ctx[b, FULL * P:SK, :]
                             ).then_inc(ctx_loaded[p], 16)

            sp.wait_ge(cleared, 2)
            load_ctx(0, 0)
            load_ctx(1, 1)
            sp.dma_start(gate_sb[:], gate_w).then_inc(experts_loaded, 16)

            def stack_keys(p):
                R = HG * DH
                for t, part in enumerate((k_hi, k_lo, k_hi, k_lo)):
                    for g in range(GROUPS):
                        sp.dma_start(k_stack[p][t * R:(t + 1) * R, g, :].bitcast(F32),
                                     part[g * R:(g + 1) * R, :].bitcast(F32)).then_inc(k_stacked, 16)

            sp.wait_ge(k_split, KSTEPS)
            stack_keys(0)

            def during(b, p):
                first = isinstance(b, int) and b == 0
                if not first:
                    sp.wait_ge(scores_ready, CHUNKS * b)
                if not (isinstance(b, int) and b + 2 >= B):
                    sp.wait_ge(scratch_filled, scratch_base(b))
                    load_ctx(b + 2, p)
                sp.wait_ge(k_split, KSTEPS * (b + 2))
                stack_keys(1 - p)

            during(0, 0)
            during(1, 1)
            with sp.Fori(1, B // 2 - 1) as i:
                during(2 * i, 0)
                during(2 * i + 1, 1)
            sp.dma_start(w1_sb[:], w1.rearrange("e d f -> d e f")).then_inc(experts_loaded, 16)
            during(B - 2, 0)
            sp.wait_ge(pv_done, CHUNKS * B)
            for e in range(E):
                sp.dma_start(w2_sb[:, e, :, :], w2[e].rearrange("(c f) d -> f c d", f=P)
                             ).then_inc(experts_loaded, 16)
            for r in range(QSTEPS):
                sp.wait_ge(y_added, E * (r + 1))
                sp.dma_start(out[r * QB:(r + 1) * QB].rearrange("b q d -> q b d"),
                             x_all[:, r * QB:(r + 1) * QB, :]).then_inc(out_stored, 16)
            sp.wait_ge(out_stored, 16 * QSTEPS)

        @block.gpsimd
        def _(pool):
            for p in range(2):
                nc.gpsimd.memset(ctx_nat[p][:, FULL, :], 0.0).then_inc(cleared, 1)
            for p in range(2):
                nc.gpsimd.memset(v_ones[p][:, 0:FULL, :, 2 * DH], 1.0).then_inc(cleared, 1)
                nc.gpsimd.memset(v_ones[p][:, FULL, :, 2 * DH], 0.0).then_inc(cleared, 1)
            pool.wait_ge(cleared, 6)
            for p in range(2):
                nc.gpsimd.memset(v_ones[p][0:TAIL, FULL, :, 2 * DH], 1.0).then_inc(cleared, 1)
            nc.gpsimd.memset(ident[:], 0.0).then_inc(ident_ready, 1)
            pool.wait_ge(ident_ready, 1)
            nc.gpsimd.affine_select(out=ident[:], in_=ident[:], compare_op=ALU.not_equal, fill=1.0,
                                    base=0, pattern=[[-1, P]], channel_multiplier=1).then_inc(ident_ready, 1)
            nc.gpsimd.iota(eids_i[:], pattern=[[1, E]], base=0, channel_multiplier=0).then_inc(iota_ready, 1)
            nc.gpsimd.memset(own_head[:], 1.0).then_inc(own_head_step, 1)
            pool.wait_ge(own_head_step, 1)
            nc.gpsimd.affine_select(out=own_head[:], in_=own_head[:], compare_op=ALU.is_ge, fill=0.0, base=0,
                                    pattern=[[-HG * DH, 4], [-DH, HG]], channel_multiplier=1
                                    ).then_inc(own_head_step, 1)
            pool.wait_ge(own_head_step, 2)
            nc.gpsimd.affine_select(out=own_head[:], in_=own_head[:], compare_op=ALU.is_ge, fill=0.0, base=DH - 1,
                                    pattern=[[HG * DH, 4], [DH, HG]], channel_multiplier=-1
                                    ).then_inc(own_head_step, 1)
            pool.wait_ge(head_mask_ready, 1)

            def stack_queries(p, b):
                pool.wait_ge(q_split, b + 1)
                if not (isinstance(b, int) and b <= 1):
                    pool.wait_ge(scores_ready, CHUNKS * (b - 1))
                nc.gpsimd.tensor_tensor(
                    q_stack[p][:], q_parts[:].bitcast(F32).unsqueeze(2).broadcast_to([P, GROUPS, HG, SQ]),
                    head_mask[:].unsqueeze(1).unsqueeze(3).broadcast_to([P, GROUPS, HG, SQ]), ALU.mult
                ).then_inc(q_stacked, 1)

            stack_queries(0, 0)
            stack_queries(1, 1)
            with pool.Fori(1, B // 2) as i:
                stack_queries(0, 2 * i)
                stack_queries(1, 2 * i + 1)

        @block.tensor
        def _(pe):
            pe.wait_ge(w_loaded, 64)
            pe.wait_ge(ident_ready, 2)
            for n in range(4):
                last = nc.tensor.transpose(scores[:, 1, 2, n * P:(n + 1) * P], w_nat[:, n, :], ident[:])
            last.then_inc(w_in_psum, 1)
            pe.wait_ge(mask_cast, 1)
            nc.tensor.transpose(scores[0:SQ, 0, 2, 0:B], mask_rows[:], ident[0:B, 0:B]).then_inc(mask_in_psum, 1)
            pe.wait_ge(w_turned_ready, 1)
            for r in range(QSTEPS):
                pe.wait_ge(normed_ready, QB * (r + 1))
                if r >= 2:
                    pe.wait_ge(xT_ready, r - 1)
                for j in range(QB):
                    last = nc.tensor.transpose(scores[:, 0, r % 2, j * SQ:(j + 1) * SQ],
                                               normed[:, r % 2, j, :], ident[0:SQ, 0:SQ])
                last.then_inc(xT_in_psum, 1)

            def turn_ctx(p, k):
                for j in range(KC):
                    last = nc.tensor.transpose(scratch[:, j * P:(j + 1) * P],
                                               ctx_nat[p][:, k * KC + j, :], ident[:])
                last.then_inc(scratch_filled, 1)

            def project_k(k):
                nc.tensor.matmul(scratch[:], w_turned[:, WK, :], ctxT[:, k * KC * P:(k + 1) * KC * P],
                                 start=True, stop=True).then_inc(scratch_filled, 1)

            def project_q(b):
                cols = slice(b * SQ, (b + 1) * SQ) if isinstance(b, int) else bass.ds(b * SQ, SQ)
                for g in range(GROUPS):
                    last = nc.tensor.matmul(scratch[:, g * SQ:(g + 1) * SQ],
                                            wq_rep[:, g, :, :].rearrange("p t r -> p (t r)"),
                                            xT[:, cols], start=True, stop=True)
                last.then_inc(scratch_filled, 1)

            def prepare(k, p, b):
                if k < QUERIES:
                    if k % 2 == 0:
                        turn_ctx(p, k // 2)
                    else:
                        project_k(k // 2)
                elif k < VALUES:
                    project_q(b)
                else:
                    project_v(k - VALUES)

            def project_v(k):
                for j in range(KC):
                    t = k * KC + j
                    last = nc.tensor.matmul(scratch[:, j * P:(j + 1) * P], ctxT[:, t * P:(t + 1) * P],
                                            w_turned[:, WV, :], start=True, stop=True)
                last.then_inc(scratch_filled, 1)

            def score_chunk(p, c):
                for m in range(CB):
                    t, g = divmod(c * CB + m, GROUPS)
                    last = nc.tensor.matmul(scores[:, c % 2, m, 0:GQ],
                                            k_stack[p][:, g, t * P:(t + 1) * P],
                                            q_stack[p][:, g, :, :].rearrange("p h q -> p (h q)"),
                                            start=True, stop=True)
                last.then_inc(scores_ready, 1)

            def weigh_values(p, c):
                for s in range(2):
                    for m in range(CB):
                        t, g = divmod(c * CB + m, GROUPS)
                        last = nc.tensor.matmul(o_sum[32 * g:32 * g + VW, s * PQ:(s + 1) * PQ],
                                                v_ones[p][:, t, 2 * g + s, :],
                                                probs[:, c % RING, m, s * PQ:(s + 1) * PQ],
                                                start=(t == 0 and s == 0), stop=(t == TILES - 1),
                                                skip_group_check=True)
                last.then_inc(pv_done, 1)

            def finish(k):
                if k == 0:
                    for n in range(4):
                        last = nc.tensor.transpose(scratch[0:SQ, n * P:(n + 1) * P],
                                                   o_raw[:, n * SQ:(n + 1) * SQ], ident[:])
                elif k == 1:
                    last = nc.tensor.transpose(scratch[:, 0:SQ], attn[:], ident[0:SQ, 0:SQ])
                else:
                    last = nc.tensor.matmul(scratch[0:SQ, 0:D], attnT[:], w_turned[:, WO, :],
                                            start=True, stop=True)
                last.then_inc(scratch_filled, 1)

            for k in range(PREP):
                if k == 0:
                    pe.wait_ge(ctx_loaded[0], 32)
                if k >= 1:
                    pe.wait_ge(scratch_emptied, k)
                if k == QUERIES:
                    pe.wait_ge(xT_ready, 1)
                    pe.wait_ge(wq_rep_ready, 1)
                prepare(k, 0, 0)
            pe.wait_ge(xT_ready, QSTEPS)
            pe.wait_ge(mask_ready, 1)
            pe.wait_ge(q_stacked, 1)
            pe.wait_ge(k_stacked, KD)
            score_chunk(0, 0)

            def attend(i, p, b, last_one):
                first = isinstance(b, int) and b == 0
                for c in range(CHUNKS):
                    if c + 1 < CHUNKS:
                        if not first or c >= 1:
                            pe.wait_ge(exp_ready, CHUNKS * b + c)
                        score_chunk(p, c + 1)
                    elif not last_one:
                        pe.wait_ge(q_stacked, b + 2)
                        pe.wait_ge(k_stacked, KD * (b + 2))
                        pe.wait_ge(exp_ready, CHUNKS * b + c)
                        score_chunk(1 - p, 0)
                    step = scratch_base(b) + c
                    if c < PREP:
                        if not last_one:
                            if c == 0:
                                pe.wait_ge(ctx_loaded[1 - p], 32 * (i + 1 + p))
                            pe.wait_ge(scratch_emptied, step)
                            prepare(c, 1 - p, b + 1)
                    elif c < PREP + FINISH and not first:
                        if c == PREP:
                            pe.wait_ge(o_taken, b)
                        pe.wait_ge(scratch_emptied, step - (PREP if last_one else 0))
                        finish(c - PREP)
                    if c >= 2 or not first:
                        pe.wait_ge(probs_ready, CHUNKS * b + c - 1)
                    if c == 2:
                        if first:
                            pe.wait_ge(o_cleared, 1)
                            pe.wait_ge(cleared, 8)
                        else:
                            pe.wait_ge(o_taken, b)
                    if c >= 2:
                        weigh_values(p, c - 2)
                    elif not first:
                        weigh_values(1 - p, CHUNKS + c - 2)

            attend(0, 0, 0, False)
            attend(0, 1, 1, False)
            with pe.Fori(1, B // 2 - 1) as i:
                attend(i, 0, 2 * i, False)
                attend(i, 1, 2 * i + 1, False)
            attend(B // 2 - 1, 0, B - 2, False)
            attend(B // 2 - 1, 1, B - 1, True)
            for c in (CHUNKS - 2, CHUNKS - 1):
                pe.wait_ge(probs_ready, CHUNKS * (B - 1) + c + 1)
                weigh_values(1, c)
            pe.wait_ge(o_taken, B)
            for k in range(FINISH):
                pe.wait_ge(scratch_emptied, scratch_base(B - 1) + FINISH + k)
                finish(k)

            pe.wait_ge(experts_loaded, 16 * (2 + E))
            for r in range(QSTEPS):
                pe.wait_ge(normed2_ready, QB * (r + 1))
                if r == 0:
                    pe.wait_ge(scratch_emptied, scratch_base(B - 1) + 2 * FINISH)
                if r >= 1:
                    pe.wait_ge(logits_ready, r)
                for j in range(QB):
                    last = nc.tensor.transpose(scratch[:, j * SQ:(j + 1) * SQ],
                                               normed[:, r % 2, j, :], ident[0:SQ, 0:SQ])
                last.then_inc(zT_in_psum, 1)
                pe.wait_ge(zT_ready, r + 1)
                for j in range(QB):
                    last = nc.tensor.matmul(scratch[0:SQ, j * E:(j + 1) * E], xT[:, (r * QB + j) * SQ:(r * QB + j + 1) * SQ],
                                            gate_sb[:], start=True, stop=True)
                last.then_inc(logits_in_psum, 1)

                def down(e):
                    n = r * E + e
                    pe.wait_ge(h_ready, 2 * (n + 1))
                    if n >= 2:
                        pe.wait_ge(y_added, n - 1)
                    yb = o_sum if n % 2 else scores[:, 1, 2, :]
                    for j in range(QB):
                        for c in range(FC):
                            last = nc.tensor.matmul(yb[0:SQ, j * D:(j + 1) * D],
                                                    h_sb[:, (2 * n + c // 2) % 4, c % 2, j * SQ:(j + 1) * SQ],
                                                    w2_sb[:, e, c, :], start=(c == 0), stop=(c == FC - 1))
                    last.then_inc(y_in_psum, 1)

                for e in range(E):
                    for half in range(2):
                        n = 2 * (r * E + e) + half
                        if n >= 2:
                            pe.wait_ge(h_ready, n - 1)
                        for c in range(2):
                            fc = half * 2 + c
                            bank = (n % 2) * 2 + c
                            last = nc.tensor.matmul(scores[:, bank // 3, bank % 3, 0:NQ],
                                                    w1_sb[:, e, fc * P:(fc + 1) * P], xT[:, r * NQ:(r + 1) * NQ],
                                                    start=True, stop=True)
                        last.then_inc(h_in_psum, 1)
                    if e >= 1:
                        down(e - 1)
                down(E - 1)

        @block.scalar
        def _(act):
            act.wait_ge(w_in_psum, 1)
            nc.scalar.copy(w_turned[:].rearrange("p n d -> p (n d)"), scores[:, 1, 2, :]
                           ).then_inc(w_turned_ready, 1)
            act.wait_ge(rstd_step, 1)
            nc.scalar.activation(std[:], var_eps[:], ACT.Sqrt).then_inc(std_ready, 1)
            act.wait_ge(w_turned_ready, 1)
            nc.scalar.copy(wq_rep[:], w_turned[:, WQ, :].rearrange("p (g r) -> p g r", g=GROUPS)
                           .unsqueeze(2).broadcast_to([P, GROUPS, 4, HG * DH])).then_inc(wq_rep_ready, 1)
            for r in range(QSTEPS):
                act.wait_ge(xT_in_psum, r + 1)
                nc.scalar.copy(xT[:, r * NQ:(r + 1) * NQ], scores[:, 0, r % 2, 0:NQ]).then_inc(xT_ready, 1)

            def prepared(k, b, step):
                first = isinstance(b, int) and b == 0
                if k > QUERIES:
                    return
                act.wait_ge(scratch_filled, step + 1)
                if k == QUERIES:
                    if not first:
                        act.wait_ge(q_split, b)
                    nc.scalar.copy(q_full[:], scratch[:, 0:GROUPS * SQ]).then_inc(scratch_emptied, 1)
                elif k % 2 == 0:
                    nc.scalar.copy(ctxT[:, k // 2 * KC * P:(k // 2 + 1) * KC * P], scratch[:]
                                   ).then_inc(scratch_emptied, 1)
                else:
                    if not first:
                        act.wait_ge(k_split, KSTEPS * (b - 1) + k // 2 + 1)
                    nc.scalar.copy(k_full[:, k // 2, :], scratch[:]).then_inc(scratch_emptied, 1)

            for k in range(PREP):
                prepared(k, 0, k)

            def attend(i, p, b, last_one):
                first = isinstance(b, int) and b == 0
                for c in range(CHUNKS):
                    act.wait_ge(scores_ready, CHUNKS * b + c + 1)
                    if not first or c >= RING:
                        act.wait_ge(pv_done, CHUNKS * b + c - RING + 1)
                    nc.scalar.activation(probs[:, c % RING, :, :], scores[:, c % 2, :, 0:GQ], ACT.Exp,
                                         scale=SCALE).then_inc(exp_ready, 1)
                    if c < PREP and not last_one:
                        prepared(c, b + 1, scratch_base(b) + c)
                    if c == PREP + 1 and not first:
                        act.wait_ge(scratch_filled, scratch_base(b) + c + 1 - (PREP if last_one else 0))
                        nc.scalar.copy(attnT[:], scratch[:, 0:SQ]).then_inc(scratch_emptied, 1)

            attend(0, 0, 0, False)
            attend(0, 1, 1, False)
            with act.Fori(1, B // 2 - 1) as i:
                attend(i, 0, 2 * i, False)
                attend(i, 1, 2 * i + 1, False)
            attend(B // 2 - 1, 0, B - 2, False)
            attend(B // 2 - 1, 1, B - 1, True)
            act.wait_ge(scratch_filled, scratch_base(B - 1) + FINISH + 2)
            nc.scalar.copy(attnT[:], scratch[:, 0:SQ]).then_inc(scratch_emptied, 1)

            act.wait_ge(rstd2_step, 1)
            nc.scalar.activation(std[:], var_eps[:], ACT.Sqrt).then_inc(std2_ready, 1)
            for r in range(QSTEPS):
                act.wait_ge(zT_in_psum, r + 1)
                nc.scalar.copy(xT[:, r * NQ:(r + 1) * NQ], scratch[:, 0:NQ]).then_inc(zT_ready, 1)
                act.wait_ge(gate_diff, r + 1)
                nc.scalar.activation(e2[:], neg_max[:], ACT.Exp).then_inc(gate_exp, 1)
                for m in range(2 * E):
                    n = 2 * E * r + m
                    act.wait_ge(h_in_psum, n + 1)
                    if n >= 4:
                        act.wait_ge(y_in_psum, n // 2 - 1)
                    bank = (n % 2) * 2
                    if bank == 0:
                        nc.scalar.activation(h_sb[:, n % 4, :, :], scores[:, 0, 0:2, 0:NQ],
                                             ACT.Gelu_apprx_tanh).then_inc(h_ready, 1)
                    else:
                        nc.scalar.activation(h_sb[:, n % 4, 0, :], scores[:, 0, 2, 0:NQ],
                                             ACT.Gelu_apprx_tanh)
                        nc.scalar.activation(h_sb[:, n % 4, 1, :], scores[:, 1, 0, 0:NQ],
                                             ACT.Gelu_apprx_tanh).then_inc(h_ready, 1)

        @block.vector
        def _(dve):
            steps = {}

            def rstd_of(step, std_sem):
                nc.vector.tensor_scalar(var_eps[:], moments[:, :, 1], EPS, None, ALU.add).then_inc(step, 1)
                dve.wait_ge(std_sem, 1)
                nc.vector.reciprocal(rstd0[:], std[:]).then_inc(step, 1)
                dve.wait_ge(step, 2)
                nc.vector.tensor_tensor(newton[:], rstd0[:], rstd0[:], ALU.mult).then_inc(step, 1)
                dve.wait_ge(step, 3)
                nc.vector.tensor_tensor(rstd[:], newton[:], var_eps[:], ALU.mult).then_inc(step, 1)
                dve.wait_ge(step, 4)
                nc.vector.tensor_scalar(newton[:], rstd[:], -0.5, 1.5, ALU.mult, ALU.add).then_inc(step, 1)
                dve.wait_ge(step, 5)
                nc.vector.tensor_tensor(rstd[:], newton[:], rstd0[:], ALU.mult).then_inc(step, 1)
                dve.wait_ge(step, 6)

            nc.vector.memset(o_sum[:], 0.0).then_inc(o_cleared, 1)
            dve.wait_ge(mask_loaded, 16)
            nc.vector.tensor_copy(mask_rows[:], mask_u8[:]).then_inc(mask_cast, 1)
            dve.wait_ge(x_loaded, 16)
            for b in range(B):
                ins = nc.vector.bn_stats(stats[:, b, :], x_all[:, b, :])
            ins.then_inc(stats_ready, 1)
            dve.wait_ge(stats_ready, 1)
            for b in range(B):
                ins = nc.vector.bn_aggr(moments[:, b, :], stats[:, b, :])
            ins.then_inc(stats_ready, 1)
            dve.wait_ge(stats_ready, 2)
            rstd_of(rstd_step, std_ready)
            def normalise(r, turned, ready):
                for j in range(QB):
                    b = r * QB + j
                    if r >= 2 and j == 0:
                        dve.wait_ge(turned, r - 1)
                    nc.vector.tensor_scalar(normed[:, r % 2, j, :], x_all[:, b, :], moments[:, b, 0:1],
                                            rstd[:, b:b + 1], ALU.subtract, ALU.mult).then_inc(ready, 1)

            for r in range(QSTEPS):
                normalise(r, xT_in_psum, normed_ready)
            dve.wait_ge(mask_in_psum, 1)
            nc.vector.tensor_copy(mask_f[:], scores[0:SQ, 0, 2, 0:B]).then_inc(mask_ready, 1)
            dve.wait_ge(own_head_step, 3)
            nc.vector.tensor_reduce(head_mask[:], own_head[:].rearrange("p t h -> p h t"), AX.X, ALU.add
                                    ).then_inc(head_mask_ready, 1)

            def split_keys(b, k, step):
                cols = slice(k * KC * P, (k + 1) * KC * P)
                dve.wait_ge(scratch_emptied, step + 1)
                if not (isinstance(b, int) and b == 0):
                    dve.wait_ge(k_stacked, KD * b)
                nc.vector.tensor_copy(k_hi[:, cols], k_full[:, k, :]).then_inc(k_hi_ready, 1)
                dve.wait_ge(k_hi_ready, KSTEPS * b + k + 1)
                nc.vector.tensor_tensor(k_lo[:, cols], k_full[:, k, :], k_hi[:, cols].bitcast(F32),
                                        ALU.subtract).then_inc(k_split, 1)

            def split_queries(b, step):
                dve.wait_ge(scratch_emptied, step + 1)
                if not (isinstance(b, int) and b == 0):
                    dve.wait_ge(q_stacked, b)
                flat = q_parts[:].rearrange("p g q -> p (g q)")
                nc.vector.tensor_copy(flat, q_full[:]).then_inc(q_hi_ready, 1)
                dve.wait_ge(q_hi_ready, b + 1)
                nc.vector.tensor_tensor(flat[P // 2:P, :], q_full[P // 2:P, :],
                                        flat[P // 2:P, :].bitcast(F32), ALU.subtract
                                        ).then_inc(q_split, 1)

            def take_values(p, k, step):
                dve.wait_ge(scratch_filled, step + 1)
                nc.vector.tensor_copy(v_ones[p][:, k * KC:(k + 1) * KC, :, 0:2 * DH],
                                      scratch[:].rearrange("p (t n d) -> p t n d", t=KC, n=PAIRS)
                                      ).then_inc(scratch_emptied, 1)

            def prepared(k, p, b, step):
                if VALUES <= k < PREP:
                    take_values(p, k - VALUES, step)
                if k <= QUERIES and k >= 2 and k % 2 == 0:
                    split_keys(b, k // 2 - 1, step - 1)
                if k == VALUES:
                    split_queries(b, step - 1)

            for k in range(PREP):
                prepared(k, 0, 0, k)

            def clip(b, c):
                dve.wait_ge(exp_ready, CHUNKS * b + c + 1)
                chunk = probs[:, c % RING, :, :].rearrange("p m q -> p (m q)")
                nc.vector.tensor_scalar(chunk, chunk, LOW, HIGH, ALU.max, ALU.min).then_inc(probs_ready, 1)

            def take_sums(b):
                dve.wait_ge(pv_done, CHUNKS * (b + 1))
                nc.vector.tensor_copy(o_raw[:], o_sum[:, 0:GQ]).then_inc(o_taken, 1)

            def finish(k, b, step):
                dve.wait_ge(scratch_filled, step + 1)
                if k == 0:
                    sums = scratch[0:SQ, :].rearrange("q (s h g w) -> q s h g w", s=2, h=2, g=GROUPS)
                    nc.vector.reciprocal(rden[:].rearrange("q (s h) g -> q s h g", s=2),
                                         sums[:, :, :, :, 2 * DH]).then_inc(rden_ready, 1)
                    dve.wait_ge(rden_ready, b + 1)
                    for h in range(2):
                        dst = attn[:].rearrange("q (g s h d) -> q s h g d", g=GROUPS, s=2, h=2)[:, :, h, :, :]
                        r = rden[:].rearrange("q (s h) g -> q s h g", s=2)[:, :, h, :]
                        ins = nc.vector.tensor_tensor(
                            dst, sums[:, :, h, :, h * DH:(h + 1) * DH],
                            r.unsqueeze(3).broadcast_to([SQ, 2, GROUPS, DH]), ALU.mult)
                    ins.then_inc(scratch_emptied, 1)
                if k == 2:
                    dve.wait_ge(mask_ready, 1)
                    xb = x_all[:, bass.ds(b, 1), :].rearrange("q o d -> q (o d)")
                    nc.vector.scalar_tensor_tensor(out=xb, in0=scratch[0:SQ, 0:D],
                                                   scalar=mask_f[:, bass.ds(b, 1)], in1=xb,
                                                   op0=ALU.mult, op1=ALU.add).then_inc(scratch_emptied, 1)
                    dve.wait_ge(scratch_emptied, step + 1)
                    nc.vector.bn_stats(stats[:, bass.ds(b, 1), :].rearrange("q o s -> q (o s)"), xb
                                       ).then_inc(x1_ready, 1)

            def attend(i, p, b, last_one):
                first = isinstance(b, int) and b == 0
                for c in range(CHUNKS):
                    if c == 2 and not first:
                        take_sums(b - 1)
                    if c >= 1:
                        clip(b, c - 1)
                    elif not first:
                        clip(b - 1, CHUNKS - 1)
                    step = scratch_base(b) + c
                    if c < PREP and not last_one:
                        prepared(c, 1 - p, b + 1, step)
                    elif PREP <= c < PREP + FINISH and not first:
                        finish(c - PREP, b - 1, step - (PREP if last_one else 0))

            attend(0, 0, 0, False)
            attend(0, 1, 1, False)
            with dve.Fori(1, B // 2 - 1) as i:
                attend(i, 0, 2 * i, False)
                attend(i, 1, 2 * i + 1, False)
            attend(B // 2 - 1, 0, B - 2, False)
            attend(B // 2 - 1, 1, B - 1, True)
            clip(B - 1, CHUNKS - 1)
            take_sums(B - 1)
            for k in range(FINISH):
                if k != 1:
                    finish(k, B - 1, scratch_base(B - 1) + FINISH + k)

            dve.wait_ge(x1_ready, B)
            for b in range(B):
                ins = nc.vector.bn_aggr(moments[:, b, :], stats[:, b, :])
            ins.then_inc(moments_ready, 1)
            dve.wait_ge(moments_ready, 1)
            rstd_of(rstd2_step, std2_ready)
            normalise(0, zT_in_psum, normed2_ready)
            dve.wait_ge(iota_ready, 1)
            nc.vector.tensor_copy(eids[:], eids_i[:]).then_inc(gate_step, 1)
            G = [1]

            def chain(ins):
                ins.then_inc(gate_step, 1)
                G[0] += 1
                dve.wait_ge(gate_step, G[0])

            for r in range(QSTEPS):
                if r + 1 < QSTEPS:
                    normalise(r + 1, zT_in_psum, normed2_ready)
                dve.wait_ge(logits_in_psum, r + 1)
                nc.vector.tensor_copy(logits, scratch[0:SQ, 0:QB * E].rearrange("q (b e) -> q b e", b=QB)
                                      ).then_inc(logits_ready, 1)
                dve.wait_ge(logits_ready, r + 1)
                for j in range(QB):
                    ins = nc.vector.max(top8[:, j, :], logits[:, j, :])
                chain(ins)
                for j in range(QB):
                    ins = nc.vector.max_index(top_at[:, j, :], top8[:, j, :], logits[:, j, :])
                chain(ins)
                chain(nc.vector.tensor_copy(top_atf, top_at[:]))
                nc.vector.tensor_tensor(neg_max[:], top8[:, :, 1], top8[:, :, 0], ALU.subtract
                                        ).then_inc(gate_diff, 1)
                dve.wait_ge(gate_exp, r + 1)
                chain(nc.vector.tensor_scalar(wsum[:], e2[:], 1.0, None, ALU.add))
                chain(nc.vector.reciprocal(wt[:, :, 0], wsum[:]))
                chain(nc.vector.tensor_tensor(wt[:, :, 1], wt[:, :, 0], e2[:], ALU.mult))
                for j in range(QB):
                    chain(nc.vector.tensor_scalar(pick[:, j, :], eids[:], top_atf[:, j, 0:1], wt[:, j, 0:1],
                                                  ALU.is_equal, ALU.mult))
                    chain(nc.vector.tensor_scalar(comb[:, j, :], eids[:], top_atf[:, j, 1:2], wt[:, j, 1:2],
                                                  ALU.is_equal, ALU.mult))
                chain(nc.vector.tensor_tensor(comb, comb, pick, ALU.add))
                for e in range(E):
                    n = r * E + e
                    dve.wait_ge(y_in_psum, n + 1)
                    yb = o_sum if n % 2 else scores[:, 1, 2, :]
                    if n >= 1:
                        dve.wait_ge(y_added, n)
                    for j in range(QB):
                        b = r * QB + j
                        ins = nc.vector.scalar_tensor_tensor(out=x_all[:, b, :], in0=yb[0:SQ, j * D:(j + 1) * D],
                                                             scalar=comb[:, j, e:e + 1], in1=x_all[:, b, :],
                                                             op0=ALU.mult, op1=ALU.add)
                    ins.then_inc(y_added, 1)


_INS = ['x', 'ctx_1024', 'mask_BxS_bf1', 'L0_xattn_W_q', 'L0_xattn_W_k', 'L0_xattn_W_v', 'L0_xattn_W_o',
        'L0_ffn_gate_w', 'L0_ffn_w1', 'L0_ffn_w2']
_OUTS = [((32, 100, 128), 'float32')]


def kernel(**inputs):
    import numpy as _np
    import concourse.bacc as _bacc
    from concourse import mybir as _mybir
    from concourse.bass_utils import run_bass_kernel_spmd as _run

    nc = _bacc.Bacc("TRN2", target_bir_lowering=False, num_devices=1)
    arrays, args = {}, []
    for name in _INS:
        a = _np.ascontiguousarray(inputs[name])
        if a.dtype == _np.bool_:
            a = a.view(_np.uint8)
        arrays[f"in_{name}_dram"] = a
        args.append(nc.dram_tensor(f"in_{name}_dram", a.shape, _mybir.dt.from_np(a.dtype), kind="ExternalInput").ap())
    for i, (shape, dtype) in enumerate(_OUTS):
        dt = _mybir.dt.from_np(_np.dtype(dtype))
        args.append(nc.dram_tensor(f"out_{i}_dram", shape, dt, kind="ExternalOutput").ap())
    xattn_moe(nc, *args)
    r = _run(nc, [arrays], core_ids=[0])
    got = tuple(r.results[0][f"out_{i}_dram"] for i in range(len(_OUTS)))
    return got[0]
```

```python
from contextlib import ExitStack
import math

import numpy as np
import concourse.bass as bass
from concourse import mybir

F32 = mybir.dt.float32
F32R = mybir.dt.float32r
U8 = mybir.dt.uint8
U32 = mybir.dt.uint32
I32 = mybir.dt.int32
ALU = mybir.AluOpType
ACT = mybir.ActivationFunctionType
AX = mybir.AxisListType

P = 128
HEADS = 16
EPS = 1e-5
CLIP = 50.0
TOP = 2


def xattn_moe(nc, x, ctx, mask, W_q, W_k, W_v, W_o, gate_w, w1, w2, out):
    B, SQ, D = x.shape
    SK = ctx.shape[1]
    E, _, F = w1.shape
    DH = D // HEADS
    TILES = -(-SK // P)
    FULL = SK // P
    TAIL = SK - FULL * P
    GROUPS = 4
    HG = HEADS // GROUPS
    GQ = HG * SQ
    PAIRS = HEADS // 2
    VW = 2 * DH + 1
    PQ = 2 * SQ
    CB = 3
    CHUNKS = TILES * GROUPS // CB
    RING = 4
    KC = 4
    KSTEPS = TILES // KC
    SCALE = 1.0 / math.sqrt(DH)
    LOW, HIGH = float(np.exp(np.float32(-CLIP))), float(np.exp(np.float32(CLIP)))
    KD = 16 * 4 * GROUPS
    QB = 4
    NQ = QB * SQ
    QSTEPS = B // QB
    FC = F // P
    CAP = B * SQ
    ROW = D + 2
    TOKEN, HOME, WEIGHT = 0, D, D + 1
    NB = 4
    YCHUNKS = 4
    YB = B // YCHUNKS
    NOWHERE = 1 << 20
    NT = (TOP * B * SQ + E * (P - 1)) // P
    assert (NT - 1) % 4 == 0 and CAP % P == 0
    assert CHUNKS == 16 and TILES == 12 and B % 2 == 0 and D == P

    PREPARE = [("query", 0)]
    for k in range(KSTEPS):
        PREPARE += [("turn", k), ("key", k)]
    PREPARE += [("value", k) for k in range(KSTEPS)]
    FINISH = [("heads", 0), ("queries", 0), ("project", 0), ("tokens", 0), ("gate", 0), ("rank", 0)]
    STEPS = PREPARE[:7] + FINISH[:3] + PREPARE[7:8] + FINISH[3:5] + PREPARE[8:] + FINISH[5:]
    IN_FIRST = [s in PREPARE for s in STEPS]
    IN_LAST = [s in FINISH for s in STEPS]
    ALONE = PREPARE[1:7] + PREPARE[:1] + PREPARE[7:]
    assert len(STEPS) == CHUNKS
    PROJECTED, GATED = STEPS.index(("project", 0)), STEPS.index(("gate", 0))

    def scratch_step(b, c):
        start = len(PREPARE)
        if isinstance(b, int) and b == 0:
            return start + sum(IN_FIRST[:c])
        before = start + sum(IN_FIRST) - len(STEPS)
        if isinstance(b, int) and b == B - 1:
            c = sum(IN_LAST[:c])
        return len(STEPS) * b + before + c

    def planned(b, c):
        if isinstance(b, int) and (b == 0 and not IN_FIRST[c] or b == B - 1 and not IN_LAST[c]):
            return None, 0
        return STEPS[c]

    def later(b, least=1):
        return not isinstance(b, int) or b >= least

    def alone(engine, told):
        engine.sem_inc(told, 1)

    es = ExitStack()
    with es:
        def sb(name, shape, dt=F32):
            return es.enter_context(nc.sbuf_tensor(name, shape, dt))

        def ps(name, shape):
            return es.enter_context(nc.psum_tensor(name, shape, F32))

        def sem(name):
            return es.enter_context(nc.semaphore(name))

        ident = sb("ident", [P, P])
        x_all = sb("x_all", [SQ, B, D])
        stats = sb("stats", [SQ, B, 6])
        moments = sb("moments", [SQ, B, 2])
        rstd = sb("rstd", [SQ, B])
        half = sb("half", [SQ, B])
        mask_u8 = sb("mask_u8", [B, SQ], U8)
        mask_rows = sb("mask_rows", [B, SQ])
        mask_f = sb("mask_f", [SQ, B])
        w_turned = sb("w_turned", [P, 4, P])
        wq_rep = sb("wq_rep", [P, GROUPS, 4, HG * DH])
        xT = sb("xT", [P, B * SQ])
        q_parts = sb("q_parts", [P, GROUPS, SQ], F32R)
        own_head = sb("own_head", [P, 4, HG])
        head_mask = sb("head_mask", [P, HG])
        q_stack = [sb(f"q_stack{p}", [P, GROUPS, HG, SQ], F32R) for p in range(2)]
        ctx_nat = [sb(f"ctx_nat{p}", [P, TILES, D]) for p in range(2)]
        ctxT = sb("ctxT", [P, TILES * P])
        k_full = sb("k_full", [P, KSTEPS, KC * P])
        q_full = sb("q_full", [P, GROUPS * SQ])
        k_hi = sb("k_hi", [P, TILES * P], F32R)
        k_lo = sb("k_lo", [P, TILES * P], F32R)
        k_stack = [sb(f"k_stack{p}", [P, GROUPS, TILES * P], F32R) for p in range(2)]
        v_both = sb("v_both", [P, 2, TILES, PAIRS, VW])
        v_ones = [v_both[:, p, :, :, :] for p in range(2)]
        probs = sb("probs", [P, RING, CB, GQ])
        normed = probs[0:SQ, 0, :, :].rearrange("q m c -> q (m c)")[:, 0:2 * QB * D].rearrange(
            "q (n j d) -> q n j d", n=2, j=QB)
        w_nat = probs[:, 1, :, :].rearrange("p m c -> p (m c)")[:, 0:4 * P].rearrange("p (n c) -> p n c", n=4)
        o_raw = sb("o_raw", [P, GQ])
        rden = sb("rden", [SQ, 4, GROUPS])
        attn = sb("attn", [SQ, D])
        attnT = sb("attnT", [P, SQ])
        stats1 = sb("stats1", [SQ, 6])
        moments1 = sb("moments1", [SQ, 2])
        rstd1 = sb("rstd1", [SQ, 2])
        rows = sb("rows", [SQ, TOP, ROW])
        zT = sb("zT", [P, SQ])
        gate_sb = sb("gate_sb", [P, E])
        logits = sb("logits", [SQ, E])
        top8 = sb("top8", [SQ, 8])
        top_at = sb("top_at", [SQ, 8], U32)
        top_atf = sb("top_atf", [SQ, TOP])
        expert_ids = sb("expert_ids", [SQ, E])
        expert_ids_i = sb("expert_ids_i", [SQ, E], I32)
        gate_diff = sb("gate_diff", [SQ, 1])
        gate_exp = sb("gate_exp", [SQ, 1])
        gate_sum = sb("gate_sum", [SQ, 1])
        picks = sb("picks", [SQ, TOP, E])
        chosen = sb("chosen", [SQ, E])
        place = sb("place", [SQ, E])
        place_of = sb("place_of", [SQ, TOP, E])
        row_at = sb("row_at", [SQ, TOP])
        row_atu = sb("row_atu", [SQ, TOP], U32)
        base_i = sb("base_i", [SQ, E], I32)
        base = sb("base", [SQ, E])
        before = sb("before", [SQ, SQ])
        ones = sb("ones", [SQ, SQ])
        home_i = sb("home_i", [SQ, TOP], I32)
        home = sb("home", [SQ, TOP])
        fill = sb("fill", [P, ROW])
        w1_sb = sb("w1_sb", [P, E, F])
        w2_sb = sb("w2_sb", [P, E, FC, D])
        first_row = sb("first_row", [1, E])
        tile_i = sb("tile_i", [1, NT], I32)
        tile_no = sb("tile_no", [1, NT])
        tiles_i = sb("tiles_i", [1, E], I32)
        tiles_s = sb("tiles_s", [1, E], I32)
        tiles_of = sb("tiles_of", [1, E])
        ends = [sb(f"ends{n}", [1, E]) for n in range(2)]
        passed, passed_tiles = [ctx_nat[1][:].rearrange("p t d -> p (t d)")[0:1, n * NT * E:(n + 1) * NT * E].rearrange("q (t e) -> q t e", e=E)
                                for n in range(2)]
        tile_passed = sb("tile_passed", [1, NT])
        tile_start = sb("tile_start", [1, NT])
        tile_shift = sb("tile_shift", [1, NT])
        tile_row = sb("tile_row", [1, NT])
        table = sb("table", [1, 2, NT], I32)
        nat = ctx_nat[0][:].rearrange("p t d -> p (t d)")
        tile_in = [nat[:, n * ROW:(n + 1) * ROW] for n in range(NB)]
        tile_out = [nat[:, NB * ROW + n * D:NB * ROW + (n + 1) * D] for n in range(NB)]
        tile_home = [sb(f"tile_home{n}", [P, 1], U32) for n in range(NB)]
        w1_tile = ctxT[:, 0:2 * F].rearrange("p (n f) -> p n f", n=2)
        tileT = ctxT[:, 2 * F:2 * F + 2 * P].rearrange("p (n r) -> p n r", n=2)
        hiddenT = k_full[:, 0:2, :].rearrange("p n (c r) -> p n c r", c=FC)
        y_all = [probs[:].rearrange("p r m q -> p (r m q)")[0:SQ, 0:B * D].rearrange("q (b d) -> q b d", b=B),
                 w1_sb[:].rearrange("p e f -> p (e f)")[0:SQ, :].rearrange("q (b d) -> q b d", b=B)]
        expert_rows = nc.dram_tensor("expert_rows", [E * CAP + P, ROW], F32, kind="Internal").ap()
        outputs = nc.dram_tensor("expert_outputs", [TOP * B * SQ, D], F32, kind="Internal").ap()

        scores = ps("scores", [P, 2, CB, 512])
        o_sum = ps("o_sum", [P, 512])
        scratch = ps("scratch", [P, 512])

        x_loaded = sem("x_loaded")
        w_loaded = sem("w_loaded")
        mask_loaded = sem("mask_loaded")
        mask_cast = sem("mask_cast")
        mask_in_psum = sem("mask_in_psum")
        mask_ready = sem("mask_ready")
        cleared = sem("cleared")
        ident_ready = sem("ident_ready")
        o_cleared = sem("o_cleared")
        stats_ready = sem("stats_ready")
        half_ready = sem("half_ready")
        rstd_step = sem("rstd_step")
        normed_ready = sem("normed_ready")
        w_in_psum = sem("w_in_psum")
        w_turned_ready = sem("w_turned_ready")
        xT_in_psum = sem("xT_in_psum")
        xT_ready = sem("xT_ready")
        wq_rep_ready = sem("wq_rep_ready")
        own_head_step = sem("own_head_step")
        head_mask_ready = sem("head_mask_ready")
        q_hi_ready = sem("q_hi_ready")
        q_stacked = sem("q_stacked")
        ctx_loaded = [sem(f"ctx_loaded{p}") for p in range(2)]
        scratch_filled = sem("scratch_filled")
        scratch_emptied = sem("scratch_emptied")
        k_hi_ready = sem("k_hi_ready")
        k_split = sem("k_split")
        q_split = sem("q_split")
        k_stacked = sem("k_stacked")
        scores_ready = sem("scores_ready")
        exp_ready = sem("exp_ready")
        probs_ready = sem("probs_ready")
        pv_done = sem("pv_done")
        o_taken = sem("o_taken")
        rden_ready = sem("rden_ready")
        stats1_ready = sem("stats1_ready")
        moments1_ready = sem("moments1_ready")
        var1_ready = sem("var1_ready")
        rstd1_ready = sem("rstd1_ready")
        rows_ready = sem("rows_ready")
        gate_loaded = sem("gate_loaded")
        top_ready = sem("top_ready")
        top_at_ready = sem("top_at_ready")
        top_atf_ready = sem("top_atf_ready")
        gate_diff_ready = sem("gate_diff_ready")
        gate_exp_ready = sem("gate_exp_ready")
        gate_sum_ready = sem("gate_sum_ready")
        weight_ready = sem("weight_ready")
        weights_ready = sem("weights_ready")
        picks_ready = sem("picks_ready")
        chosen_ready = sem("chosen_ready")
        place_ready = sem("place_ready")
        place_of_ready = sem("place_of_ready")
        row_at_ready = sem("row_at_ready")
        routes_ready = sem("routes_ready")
        homes_written = sem("homes_written")
        homes_next = sem("homes_next")
        before_step = sem("before_step")
        rows_ones_ready = sem("rows_ones_ready")
        ids_step = sem("ids_step")
        fill_step = sem("fill_step")
        rows_filled = sem("rows_filled")
        spare_rows_filled = sem("spare_rows_filled")
        rows_sent = sem("rows_sent")
        x1_ready = sem("x1_ready")
        w_experts_loaded = sem("w_experts_loaded")
        table_step = sem("table_step")
        table_ready = sem("table_ready")
        tile_turned = sem("tile_turned")
        tileT_ready = sem("tileT_ready")
        w1_ready = sem("w1_ready")
        hidden_in_psum = sem("hidden_in_psum")
        hidden_ready = sem("hidden_ready")
        y_in_psum = sem("y_in_psum")
        home_ready = sem("home_ready")
        y_ready = sem("y_ready")
        y_step = sem("y_step")
        out_ready = sem("out_ready")
        out_stored = sem("out_stored")
        tile_loaded = [sem(f"tile_loaded{n}") for n in range(NB)]
        y_sent = [sem(f"y_sent{n}") for n in range(NB)]
        y_loaded = [sem(f"y_loaded{n}") for n in range(YCHUNKS)]

        dve_passed = sem("dve_passed")
        pool_passed = sem("pool_passed")
        sp_passed = sem("sp_passed")

        WQ, WK, WV, WO = range(4)

        block = es.enter_context(nc.Block())

        @block.sync
        def _(sp):
            sp.dma_start(x_all[:], x.rearrange("b q d -> q b d")).then_inc(x_loaded, 16)
            for n, w in enumerate((W_q, W_k, W_v, W_o)):
                sp.dma_start(w_nat[:, n, :], w).then_inc(w_loaded, 16)
            sp.dma_start(mask_u8[:], mask).then_inc(mask_loaded, 16)

            def load_ctx(b, p):
                sp.dma_start(ctx_nat[p][:, 0:FULL, :],
                             ctx[b, 0:FULL * P, :].rearrange("(p t) d -> p t d", t=FULL)
                             ).then_inc(ctx_loaded[p], 16)
                sp.dma_start(ctx_nat[p][0:TAIL, FULL, :], ctx[b, FULL * P:SK, :]
                             ).then_inc(ctx_loaded[p], 16)

            sp.wait_ge(cleared, 2)
            load_ctx(0, 0)
            load_ctx(1, 1)
            sp.dma_start(gate_sb[:], gate_w).then_inc(gate_loaded, 16)

            def fill_rows(b):
                if later(b):
                    sp.wait_ge(rows_filled, 16 * b)
                sp.dma_start(expert_rows[0:E * CAP, :].rearrange("(e r) c -> r e c", e=E)[bass.ds(b * SQ, SQ)],
                             fill[0:SQ, :].unsqueeze(1).broadcast_to([SQ, E, ROW])).then_inc(rows_filled, 16)

            sp.wait_ge(fill_step, 2)
            sp.dma_start(expert_rows[E * CAP:E * CAP + P, :], fill[:]).then_inc(spare_rows_filled, 16)
            fill_rows(0)

            def stack_keys(p):
                R = HG * DH
                for t, part in enumerate((k_hi, k_lo, k_hi, k_lo)):
                    for g in range(GROUPS):
                        sp.dma_start(k_stack[p][t * R:(t + 1) * R, g, :].bitcast(F32),
                                     part[g * R:(g + 1) * R, :].bitcast(F32)).then_inc(k_stacked, 16)

            sp.wait_ge(k_split, KSTEPS)
            stack_keys(0)

            def during(b, p):
                if later(b):
                    sp.wait_ge(scores_ready, CHUNKS * b)
                    alone(sp, sp_passed)
                if not (isinstance(b, int) and b + 2 >= B):
                    sp.wait_ge(scratch_filled, scratch_step(b, 0))
                    load_ctx(b + 2, p)
                fill_rows(b + 1)
                sp.wait_ge(k_split, KSTEPS * (b + 2))
                stack_keys(1 - p)

            during(0, 0)
            during(1, 1)
            with sp.Fori(1, B // 2 - 1) as i:
                during(2 * i, 0)
                during(2 * i + 1, 1)
            during(B - 2, 0)
            sp.dma_start(w1_sb[:], w1.rearrange("e d f -> d e f")).then_inc(w_experts_loaded, 16)
            for e in range(E):
                sp.dma_start(w2_sb[:, e, :, :], w2[e].rearrange("(c f) d -> f c d", f=P)
                             ).then_inc(w_experts_loaded, 16)

            sp.wait_ge(rows_sent, 16 * TOP * B)
            sp.wait_ge(spare_rows_filled, 16)
            sp.wait_ge(table_ready, 1)

            def load_tile(t, n):
                if not isinstance(t, int) or t >= NB:
                    sp.wait_ge(y_ready, t - NB + 1)
                row = sp.value_load(table[0:1, 1, bass.ds(t, 1)], min_val=0, max_val=E * CAP)
                sp.dma_start(tile_in[n], expert_rows[bass.ds(row, P), :]).then_inc(tile_loaded[n], 16)

            for t in range(NB):
                load_tile(t, t)
            with sp.Fori(1, NT // NB) as i:
                for n in range(NB):
                    load_tile(NB * i + n, n)
            load_tile(NT - 1, 0)

            for n in range(NB):
                sp.wait_ge(y_sent[n], 16 * (NT // NB + (n == 0)))
            for c in range(YCHUNKS):
                for k in range(TOP):
                    first_row_of = (k * B + c * YB) * SQ
                    sp.dma_start(y_all[k][:, c * YB:(c + 1) * YB, :],
                                 outputs[first_row_of:first_row_of + YB * SQ, :].rearrange("(b q) d -> q b d", q=SQ)
                                 ).then_inc(y_loaded[c], 16)
            for c in range(YCHUNKS):
                sp.wait_ge(out_ready, c + 1)
                sp.dma_start(out[c * YB:(c + 1) * YB].rearrange("b q d -> q b d"),
                             x_all[:, c * YB:(c + 1) * YB, :]).then_inc(out_stored, 16)
            sp.wait_ge(out_stored, 16 * YCHUNKS)

        @block.gpsimd
        def _(pool):
            for p in range(2):
                nc.gpsimd.memset(ctx_nat[p][:, FULL, :], 0.0).then_inc(cleared, 1)
            nc.gpsimd.memset(half[:], -0.5).then_inc(half_ready, 1)
            for p in range(2):
                nc.gpsimd.memset(v_ones[p][:, 0:FULL, :, 2 * DH], 1.0).then_inc(cleared, 1)
                nc.gpsimd.memset(v_ones[p][:, FULL, :, 2 * DH], 0.0).then_inc(cleared, 1)
            pool.wait_ge(cleared, 6)
            for p in range(2):
                nc.gpsimd.memset(v_ones[p][0:TAIL, FULL, :, 2 * DH], 1.0).then_inc(cleared, 1)
            nc.gpsimd.memset(ident[:], 0.0).then_inc(ident_ready, 1)
            pool.wait_ge(ident_ready, 1)
            nc.gpsimd.affine_select(out=ident[:], in_=ident[:], compare_op=ALU.not_equal, fill=1.0,
                                    base=0, pattern=[[-1, P]], channel_multiplier=1).then_inc(ident_ready, 1)
            pool.wait_ge(stats_ready, 2)
            pool.wait_ge(half_ready, 1)
            nc.gpsimd.tensor_scalar(rstd[:], moments[:, :, 1], EPS, None, ALU.add).then_inc(rstd_step, 1)
            pool.wait_ge(rstd_step, 1)
            nc.gpsimd.tensor_tensor(rstd[:], rstd[:], half[:], ALU.pow).then_inc(rstd_step, 1)
            nc.gpsimd.memset(own_head[:], 1.0).then_inc(own_head_step, 1)
            pool.wait_ge(own_head_step, 1)
            nc.gpsimd.affine_select(out=own_head[:], in_=own_head[:], compare_op=ALU.is_ge, fill=0.0, base=0,
                                    pattern=[[-HG * DH, 4], [-DH, HG]], channel_multiplier=1
                                    ).then_inc(own_head_step, 1)
            pool.wait_ge(own_head_step, 2)
            nc.gpsimd.affine_select(out=own_head[:], in_=own_head[:], compare_op=ALU.is_ge, fill=0.0, base=DH - 1,
                                    pattern=[[HG * DH, 4], [DH, HG]], channel_multiplier=-1
                                    ).then_inc(own_head_step, 1)
            nc.gpsimd.memset(fill[:], 0.0).then_inc(fill_step, 1)
            pool.wait_ge(fill_step, 1)
            nc.gpsimd.memset(fill[:, HOME:HOME + 1], float(NOWHERE)).then_inc(fill_step, 1)
            nc.gpsimd.memset(before[:], 1.0).then_inc(before_step, 1)
            pool.wait_ge(before_step, 1)
            nc.gpsimd.affine_select(out=before[:], in_=before[:], compare_op=ALU.is_ge, fill=0.0, base=-1,
                                    pattern=[[1, SQ]], channel_multiplier=-1).then_inc(before_step, 1)
            nc.gpsimd.memset(ones[:], 1.0).then_inc(rows_ones_ready, 1)
            nc.gpsimd.iota(expert_ids_i[:], pattern=[[1, E]], base=0, channel_multiplier=0).then_inc(ids_step, 1)
            nc.gpsimd.iota(base_i[:], pattern=[[CAP, E]], base=0, channel_multiplier=0).then_inc(ids_step, 1)
            nc.gpsimd.iota(home_i[:], pattern=[[B * SQ, TOP]], base=0, channel_multiplier=1).then_inc(ids_step, 1)
            nc.gpsimd.iota(tile_i[:], pattern=[[1, NT]], base=0, channel_multiplier=0).then_inc(ids_step, 1)
            pool.wait_ge(head_mask_ready, 1)

            def stack_queries(p, b):
                pool.wait_ge(q_split, b + 1)
                if later(b, 2):
                    pool.wait_ge(scores_ready, CHUNKS * (b - 1))
                nc.gpsimd.tensor_tensor(
                    q_stack[p][:], q_parts[:].bitcast(F32).unsqueeze(2).broadcast_to([P, GROUPS, HG, SQ]),
                    head_mask[:].unsqueeze(1).unsqueeze(3).broadcast_to([P, GROUPS, HG, SQ]), ALU.mult
                ).then_inc(q_stacked, 1)

            def route(f):
                pool.wait_ge(homes_next, f + 1)
                if later(f):
                    pool.wait_ge(rows_sent, 16 * TOP * f)
                alone(pool, pool_passed)
                nc.gpsimd.tensor_copy(rows[:, :, HOME], home[:]).then_inc(homes_written, 1)
                pool.wait_ge(homes_written, f + 1)
                alone(pool, pool_passed)
                nc.gpsimd.tensor_scalar(home[:], home[:], float(SQ), None, ALU.add).then_inc(homes_next, 1)
                pool.wait_ge(moments1_ready, f + 1)
                alone(pool, pool_passed)
                nc.gpsimd.tensor_scalar(rstd1[:, 0:1], moments1[:, 1:2], EPS, None, ALU.add).then_inc(var1_ready, 1)
                pool.wait_ge(var1_ready, f + 1)
                nc.gpsimd.tensor_tensor(rstd1[:, 1:2], rstd1[:, 0:1], half[:, 0:1], ALU.pow).then_inc(rstd1_ready, 1)
                pool.wait_ge(routes_ready, f + 1)
                pool.wait_ge(rows_filled, 16 * (f + 1))
                alone(pool, pool_passed)
                for k in range(TOP):
                    nc.gpsimd.indirect_dma_start(
                        out=expert_rows[0:E * CAP, :], out_offset=bass.IndirectOffsetOnAxis(ap=row_atu[:, k:k + 1], axis=0),
                        in_=rows[:, k, :], in_offset=None).then_inc(rows_sent, 16)

            stack_queries(0, 0)
            stack_queries(1, 1)
            stack_queries(0, 2)
            route(0)
            with pool.Fori(1, B // 2 - 1) as i:
                stack_queries(1, 2 * i + 1)
                route(2 * i - 1)
                stack_queries(0, 2 * i + 2)
                route(2 * i)
            stack_queries(1, B - 1)
            for f in range(B - 3, B):
                route(f)

            def send(t, n):
                pool.wait_ge(y_ready, t + 1)
                alone(pool, pool_passed)
                nc.gpsimd.indirect_dma_start(
                    out=outputs[:, :], out_offset=bass.IndirectOffsetOnAxis(ap=tile_home[n][:], axis=0),
                    in_=tile_out[n], in_offset=None, bounds_check=TOP * B * SQ - 1, oob_is_err=False
                ).then_inc(y_sent[n], 16)

            with pool.Fori(0, NT // NB) as i:
                for n in range(NB):
                    send(NB * i + n, n)
            send(NT - 1, 0)

        @block.tensor
        def _(pe):
            pe.wait_ge(w_loaded, 64)
            pe.wait_ge(ident_ready, 2)
            for n in range(4):
                last = nc.tensor.transpose(scores[:, 1, 2, n * P:(n + 1) * P], w_nat[:, n, :], ident[:])
            last.then_inc(w_in_psum, 1)
            pe.wait_ge(mask_cast, 1)
            nc.tensor.transpose(scores[0:SQ, 0, 2, 0:B], mask_rows[:], ident[0:B, 0:B]).then_inc(mask_in_psum, 1)
            pe.wait_ge(w_turned_ready, 1)
            for r in range(QSTEPS):
                pe.wait_ge(normed_ready, QB * (r + 1))
                if r >= 2:
                    pe.wait_ge(xT_ready, r - 1)
                for j in range(QB):
                    last = nc.tensor.transpose(scores[:, 0, r % 2, j * SQ:(j + 1) * SQ],
                                               normed[:, r % 2, j, :], ident[0:SQ, 0:SQ])
                last.then_inc(xT_in_psum, 1)

            def turn_ctx(p, k):
                for j in range(KC):
                    last = nc.tensor.transpose(scratch[:, j * P:(j + 1) * P],
                                               ctx_nat[p][:, k * KC + j, :], ident[:])
                return last

            def project_k(k):
                return nc.tensor.matmul(scratch[:], w_turned[:, WK, :], ctxT[:, k * KC * P:(k + 1) * KC * P],
                                        start=True, stop=True)

            def project_q(b):
                cols = slice(b * SQ, (b + 1) * SQ) if isinstance(b, int) else bass.ds(b * SQ, SQ)
                for g in range(GROUPS):
                    last = nc.tensor.matmul(scratch[:, g * SQ:(g + 1) * SQ],
                                            wq_rep[:, g, :, :].rearrange("p t r -> p (t r)"),
                                            xT[:, cols], start=True, stop=True)
                return last

            def project_v(k):
                for j in range(KC):
                    t = k * KC + j
                    last = nc.tensor.matmul(scratch[:, j * P:(j + 1) * P], ctxT[:, t * P:(t + 1) * P],
                                            w_turned[:, WV, :], start=True, stop=True)
                return last

            def into_scratch(name, k, p, b, f, step):
                pe.wait_ge(scratch_emptied, step)
                if name == "query":
                    last = project_q(b)
                elif name == "turn":
                    last = turn_ctx(p, k)
                elif name == "key":
                    last = project_k(k)
                elif name == "value":
                    last = project_v(k)
                elif name == "heads":
                    pe.wait_ge(o_taken, f + 1)
                    for n in range(4):
                        last = nc.tensor.transpose(scratch[0:SQ, n * P:(n + 1) * P],
                                                   o_raw[:, n * SQ:(n + 1) * SQ], ident[:])
                elif name == "queries":
                    last = nc.tensor.transpose(scratch[:, 0:SQ], attn[:], ident[0:SQ, 0:SQ])
                elif name == "project":
                    last = nc.tensor.matmul(scratch[0:SQ, 0:D], attnT[:], w_turned[:, WO, :],
                                            start=True, stop=True)
                elif name == "tokens":
                    pe.wait_ge(rows_ready, f + 1)
                    last = nc.tensor.transpose(scratch[:, 0:SQ], rows[:, 0, TOKEN:D], ident[0:SQ, 0:SQ])
                elif name == "gate":
                    if isinstance(f, int) and f == 0:
                        pe.wait_ge(gate_loaded, 16)
                    last = nc.tensor.matmul(scratch[0:SQ, 0:E], zT[:], gate_sb[:], start=True, stop=True)
                else:
                    pe.wait_ge(chosen_ready, f + 1)
                    if isinstance(f, int) and f == 0:
                        pe.wait_ge(before_step, 2)
                        pe.wait_ge(rows_ones_ready, 1)
                    nc.tensor.matmul(scratch[0:SQ, 0:E], before[:], chosen[:], start=True, stop=True)
                    last = nc.tensor.matmul(scratch[0:SQ, E:2 * E], ones[:], chosen[:], start=True, stop=True)
                last.then_inc(scratch_filled, 1)

            def score_chunk(p, c):
                for m in range(CB):
                    t, g = divmod(c * CB + m, GROUPS)
                    last = nc.tensor.matmul(scores[:, c % 2, m, 0:GQ],
                                            k_stack[p][:, g, t * P:(t + 1) * P],
                                            q_stack[p][:, g, :, :].rearrange("p h q -> p (h q)"),
                                            start=True, stop=True)
                last.then_inc(scores_ready, 1)

            def weigh_values(p, c):
                for s in range(2):
                    for m in range(CB):
                        t, g = divmod(c * CB + m, GROUPS)
                        last = nc.tensor.matmul(o_sum[32 * g:32 * g + VW, s * PQ:(s + 1) * PQ],
                                                v_ones[p][:, t, 2 * g + s, :],
                                                probs[:, c % RING, m, s * PQ:(s + 1) * PQ],
                                                start=(t == 0 and s == 0), stop=(t == TILES - 1),
                                                skip_group_check=True)
                last.then_inc(pv_done, 1)

            for step, (name, k) in enumerate(ALONE):
                if step == 0:
                    pe.wait_ge(ctx_loaded[0], 32)
                if name == "query":
                    pe.wait_ge(xT_ready, 1)
                    pe.wait_ge(wq_rep_ready, 1)
                into_scratch(name, k, 0, 0, None, step)
            pe.wait_ge(xT_ready, QSTEPS)
            pe.wait_ge(mask_ready, 1)
            pe.wait_ge(q_stacked, 1)
            pe.wait_ge(k_stacked, KD)
            score_chunk(0, 0)

            def attend(i, p, b, last_one):
                for c in range(CHUNKS):
                    if c + 1 < CHUNKS:
                        if later(b) or c >= 1:
                            pe.wait_ge(exp_ready, CHUNKS * b + c)
                        score_chunk(p, c + 1)
                    elif not last_one:
                        pe.wait_ge(q_stacked, b + 2)
                        pe.wait_ge(k_stacked, KD * (b + 2))
                        pe.wait_ge(exp_ready, CHUNKS * b + c)
                        score_chunk(1 - p, 0)
                    name, k = planned(b, c)
                    if name == "turn" and k == 0:
                        pe.wait_ge(ctx_loaded[1 - p], 32 * (i + 1 + p))
                    if name:
                        into_scratch(name, k, 1 - p, b + 1, b - 1, scratch_step(b, c))
                    if c >= 2 or later(b):
                        pe.wait_ge(probs_ready, CHUNKS * b + c - 1)
                    if c == 2:
                        if later(b):
                            pe.wait_ge(o_taken, b)
                        else:
                            pe.wait_ge(o_cleared, 1)
                            pe.wait_ge(cleared, 8)
                    if c >= 2:
                        weigh_values(p, c - 2)
                    elif later(b):
                        weigh_values(1 - p, CHUNKS + c - 2)

            attend(0, 0, 0, False)
            attend(0, 1, 1, False)
            with pe.Fori(1, B // 2 - 1) as i:
                attend(i, 0, 2 * i, False)
                attend(i, 1, 2 * i + 1, False)
            attend(B // 2 - 1, 0, B - 2, False)
            attend(B // 2 - 1, 1, B - 1, True)
            for c in (CHUNKS - 2, CHUNKS - 1):
                pe.wait_ge(probs_ready, CHUNKS * (B - 1) + c + 1)
                weigh_values(1, c)
            for n, (name, k) in enumerate(FINISH):
                into_scratch(name, k, None, None, B - 1, scratch_step(B - 1, CHUNKS) + n)

            pe.wait_ge(scratch_emptied, scratch_step(B - 1, CHUNKS) + len(FINISH))
            pe.wait_ge(table_ready, 1)
            pe.wait_ge(w_experts_loaded, 16 * (1 + E))

            def turn_tile(t, n, i):
                pe.wait_ge(tile_loaded[n], 16 * (i + 1))
                if not isinstance(t, int) or t >= 2:
                    pe.wait_ge(tileT_ready, t - 1)
                nc.tensor.transpose(scores[:, n % 2, 2, 0:P], tile_in[n][:, TOKEN:D], ident[:]
                                    ).then_inc(tile_turned, 1)

            def up(t, n):
                pe.wait_ge(tileT_ready, t + 1)
                pe.wait_ge(w1_ready, t + 1)
                if not isinstance(t, int) or t >= 2:
                    pe.wait_ge(hidden_ready, t - 1)
                for c in range(FC):
                    last = nc.tensor.matmul(scores[:, n % 2, 0, c * P:(c + 1) * P],
                                            w1_tile[:, n % 2, c * P:(c + 1) * P], tileT[:, n % 2, :],
                                            start=True, stop=True)
                last.then_inc(hidden_in_psum, 1)

            def down(t, n):
                expert = pe.value_load(table[0:1, 0, bass.ds(t, 1)], min_val=0, max_val=E - 1)
                pe.wait_ge(hidden_ready, t + 1)
                if not isinstance(t, int) or t >= 2:
                    pe.wait_ge(y_ready, t - 1)
                for c in range(FC):
                    last = nc.tensor.matmul(scores[:, n % 2, 1, 0:D], hiddenT[:, n % 2, c, :],
                                            w2_sb[:, bass.ds(expert, 1), c, :].rearrange("f o d -> f (o d)"),
                                            start=(c == 0), stop=(c == FC - 1))
                last.then_inc(y_in_psum, 1)

            turn_tile(0, 0, 0)

            def tile(t, n, i):
                if not (isinstance(t, int) and t == NT - 1):
                    turn_tile(t + 1, (n + 1) % NB, i + (n + 1) // NB)
                up(t, n)
                if not (isinstance(t, int) and t == 0):
                    down(t - 1, (n - 1) % NB)

            for n in range(NB):
                tile(n, n, 0)
            with pe.Fori(1, NT // NB) as i:
                for n in range(NB):
                    tile(NB * i + n, n, i)
            tile(NT - 1, 0, NT // NB)
            down(NT - 1, 0)

        @block.scalar
        def _(act):
            act.wait_ge(w_in_psum, 1)
            nc.scalar.copy(w_turned[:].rearrange("p n d -> p (n d)"), scores[:, 1, 2, :]
                           ).then_inc(w_turned_ready, 1)
            act.wait_ge(w_turned_ready, 1)
            nc.scalar.copy(wq_rep[:], w_turned[:, WQ, :].rearrange("p (g r) -> p g r", g=GROUPS)
                           .unsqueeze(2).broadcast_to([P, GROUPS, 4, HG * DH])).then_inc(wq_rep_ready, 1)

            for r in range(QSTEPS):
                act.wait_ge(xT_in_psum, r + 1)
                nc.scalar.copy(xT[:, r * NQ:(r + 1) * NQ], scores[:, 0, r % 2, 0:NQ]).then_inc(xT_ready, 1)

            def take(name, k, b, f, step):
                if name not in ("turn", "key", "query", "queries", "tokens"):
                    return
                act.wait_ge(scratch_filled, step + 1)
                if name == "turn":
                    nc.scalar.copy(ctxT[:, k * KC * P:(k + 1) * KC * P], scratch[:]).then_inc(scratch_emptied, 1)
                elif name == "key":
                    if later(b):
                        act.wait_ge(k_split, KSTEPS * (b - 1) + k + 1)
                    nc.scalar.copy(k_full[:, k, :], scratch[:]).then_inc(scratch_emptied, 1)
                elif name == "query":
                    if later(b):
                        act.wait_ge(q_split, b)
                    nc.scalar.copy(q_full[:], scratch[:, 0:GROUPS * SQ]).then_inc(scratch_emptied, 1)
                elif name == "queries":
                    nc.scalar.copy(attnT[:], scratch[:, 0:SQ]).then_inc(scratch_emptied, 1)
                else:
                    nc.scalar.copy(zT[:], scratch[:, 0:SQ]).then_inc(scratch_emptied, 1)

            def second_share(f):
                act.wait_ge(gate_diff_ready, f + 1)
                nc.scalar.activation(gate_exp[:], gate_diff[:], ACT.Exp).then_inc(gate_exp_ready, 1)

            for step, (name, k) in enumerate(ALONE):
                take(name, k, 0, None, step)

            def attend(b):
                for c in range(CHUNKS):
                    act.wait_ge(scores_ready, CHUNKS * b + c + 1)
                    if later(b) or c >= RING:
                        act.wait_ge(pv_done, CHUNKS * b + c - RING + 1)
                    nc.scalar.activation(probs[:, c % RING, :, :], scores[:, c % 2, :, 0:GQ], ACT.Exp,
                                         scale=SCALE).then_inc(exp_ready, 1)
                    name, k = planned(b, c)
                    take(name, k, b + 1, b - 1, scratch_step(b, c))
                    if c == GATED + 2 and later(b):
                        second_share(b - 1)

            attend(0)
            attend(1)
            with act.Fori(1, B // 2 - 1) as i:
                attend(2 * i)
                attend(2 * i + 1)
            attend(B - 2)
            attend(B - 1)
            for n, (name, k) in enumerate(FINISH):
                take(name, k, None, B - 1, scratch_step(B - 1, CHUNKS) + n)
            second_share(B - 1)

            def take_tile(t, n):
                act.wait_ge(tile_turned, t + 1)
                if not isinstance(t, int) or t >= 2:
                    act.wait_ge(hidden_in_psum, t - 1)
                nc.scalar.copy(tileT[:, n % 2, :], scores[:, n % 2, 2, 0:P]).then_inc(tileT_ready, 1)

            def gelu(t, n):
                act.wait_ge(hidden_in_psum, t + 1)
                if not isinstance(t, int) or t >= 2:
                    act.wait_ge(y_in_psum, t - 1)
                nc.scalar.activation(hiddenT[:, n % 2, :, :], scores[:, n % 2, 0, :].rearrange("p (c r) -> p c r", c=FC),
                                     ACT.Gelu_apprx_tanh).then_inc(hidden_ready, 1)

            take_tile(0, 0)

            def tile(t, n):
                if not (isinstance(t, int) and t == NT - 1):
                    take_tile(t + 1, n + 1)
                gelu(t, n)

            for n in range(NB):
                tile(n, n)
            with act.Fori(1, NT // NB) as i:
                for n in range(NB):
                    tile(NB * i + n, n)
            tile(NT - 1, 0)

        @block.vector
        def _(dve):
            nc.vector.memset(o_sum[:], 0.0).then_inc(o_cleared, 1)
            dve.wait_ge(mask_loaded, 16)
            nc.vector.tensor_copy(mask_rows[:], mask_u8[:]).then_inc(mask_cast, 1)
            dve.wait_ge(x_loaded, 16)
            for b in range(B):
                ins = nc.vector.bn_stats(stats[:, b, :], x_all[:, b, :])
            ins.then_inc(stats_ready, 1)
            dve.wait_ge(stats_ready, 1)
            for b in range(B):
                ins = nc.vector.bn_aggr(moments[:, b, :], stats[:, b, :])
            ins.then_inc(stats_ready, 1)
            dve.wait_ge(rstd_step, 2)
            for r in range(QSTEPS):
                for j in range(QB):
                    b = r * QB + j
                    if r >= 2 and j == 0:
                        dve.wait_ge(xT_in_psum, r - 1)
                    nc.vector.tensor_scalar(normed[:, r % 2, j, :], x_all[:, b, :], moments[:, b, 0:1],
                                            rstd[:, b:b + 1], ALU.subtract, ALU.mult).then_inc(normed_ready, 1)
            dve.wait_ge(mask_in_psum, 1)
            nc.vector.tensor_copy(mask_f[:], scores[0:SQ, 0, 2, 0:B]).then_inc(mask_ready, 1)
            dve.wait_ge(own_head_step, 3)
            nc.vector.tensor_reduce(head_mask[:], own_head[:].rearrange("p t h -> p h t"), AX.X, ALU.add
                                    ).then_inc(head_mask_ready, 1)

            def split_keys(b, k, step):
                cols = slice(k * KC * P, (k + 1) * KC * P)
                dve.wait_ge(scratch_emptied, step + 1)
                if later(b):
                    dve.wait_ge(k_stacked, KD * b)
                nc.vector.tensor_copy(k_hi[:, cols], k_full[:, k, :]).then_inc(k_hi_ready, 1)
                dve.wait_ge(k_hi_ready, KSTEPS * b + k + 1)
                nc.vector.tensor_tensor(k_lo[:, cols], k_full[:, k, :], k_hi[:, cols].bitcast(F32),
                                        ALU.subtract).then_inc(k_split, 1)

            def split_queries(b, step):
                dve.wait_ge(scratch_emptied, step + 1)
                if later(b):
                    dve.wait_ge(q_stacked, b)
                flat = q_parts[:].rearrange("p g q -> p (g q)")
                nc.vector.tensor_copy(flat, q_full[:]).then_inc(q_hi_ready, 1)
                dve.wait_ge(q_hi_ready, b + 1)
                nc.vector.tensor_tensor(flat[P // 2:P, :], q_full[P // 2:P, :],
                                        flat[P // 2:P, :].bitcast(F32), ALU.subtract
                                        ).then_inc(q_split, 1)

            def split(name, k, b, step):
                if name == "key":
                    split_keys(b, k, step)
                if name == "query":
                    split_queries(b, step)

            def take_values(p, k, step):
                dve.wait_ge(scratch_filled, step + 1)
                nc.vector.tensor_copy(v_ones[p][:, k * KC:(k + 1) * KC, :, 0:2 * DH],
                                      scratch[:].rearrange("p (t n d) -> p t n d", t=KC, n=PAIRS)
                                      ).then_inc(scratch_emptied, 1)

            for step, (name, k) in enumerate(ALONE):
                if step:
                    split(*ALONE[step - 1], 0, step - 1)
                if name == "value":
                    take_values(0, k, step)
            dve.wait_ge(ids_step, 4)
            nc.vector.tensor_copy(expert_ids[:], expert_ids_i[:]).then_inc(ids_step, 1)
            nc.vector.tensor_copy(base[:], base_i[:]).then_inc(ids_step, 1)
            nc.vector.tensor_copy(first_row[:], base_i[0:1, :]).then_inc(ids_step, 1)
            nc.vector.tensor_copy(home[:], home_i[:]).then_inc(homes_next, 1)
            nc.vector.tensor_copy(tile_no[:], tile_i[:]).then_inc(ids_step, 1)
            dve.wait_ge(ids_step, 8)

            def clip(b, c):
                dve.wait_ge(exp_ready, CHUNKS * b + c + 1)
                chunk = probs[:, c % RING, :, :].rearrange("p m q -> p (m q)")
                nc.vector.tensor_scalar(chunk, chunk, LOW, HIGH, ALU.max, ALU.min).then_inc(probs_ready, 1)

            def take_sums(b):
                dve.wait_ge(pv_done, CHUNKS * (b + 1))
                nc.vector.tensor_copy(o_raw[:], o_sum[:, 0:GQ]).then_inc(o_taken, 1)

            def heads(f, step):
                dve.wait_ge(scratch_filled, step + 1)
                sums = scratch[0:SQ, :].rearrange("q (s h g w) -> q s h g w", s=2, h=2, g=GROUPS)
                nc.vector.reciprocal(rden[:].rearrange("q (s h) g -> q s h g", s=2),
                                     sums[:, :, :, :, 2 * DH]).then_inc(rden_ready, 1)
                dve.wait_ge(rden_ready, f + 1)
                for h in range(2):
                    dst = attn[:].rearrange("q (g s h d) -> q s h g d", g=GROUPS, s=2, h=2)[:, :, h, :, :]
                    r = rden[:].rearrange("q (s h) g -> q s h g", s=2)[:, :, h, :]
                    ins = nc.vector.tensor_tensor(
                        dst, sums[:, :, h, :, h * DH:(h + 1) * DH],
                        r.unsqueeze(3).broadcast_to([SQ, 2, GROUPS, DH]), ALU.mult)
                ins.then_inc(scratch_emptied, 1)

            def tokens_of(f):
                return x_all[:, bass.ds(f, 1), :].rearrange("q o d -> q (o d)")

            def project(f, step):
                dve.wait_ge(scratch_filled, step + 1)
                if isinstance(f, int) and f == 0:
                    dve.wait_ge(mask_ready, 1)
                nc.vector.scalar_tensor_tensor(out=tokens_of(f), in0=scratch[0:SQ, 0:D],
                                               scalar=mask_f[:, bass.ds(f, 1)], in1=tokens_of(f),
                                               op0=ALU.mult, op1=ALU.add).then_inc(scratch_emptied, 1)
                dve.wait_ge(scratch_emptied, step + 1)
                alone(dve, dve_passed)
                nc.vector.bn_stats(stats1[:], tokens_of(f)).then_inc(stats1_ready, 1)
                dve.wait_ge(stats1_ready, f + 1)
                alone(dve, dve_passed)
                nc.vector.bn_aggr(moments1[:], stats1[:]).then_inc(moments1_ready, 1)

            def norm_tokens(f):
                dve.wait_ge(rstd1_ready, f + 1)
                if later(f):
                    dve.wait_ge(rows_sent, 16 * TOP * f)
                for k in range(TOP):
                    ins = nc.vector.tensor_scalar(rows[:, k, TOKEN:D], tokens_of(f), moments1[:, 0:1],
                                                  rstd1[:, 1:2], ALU.subtract, ALU.mult)
                ins.then_inc(rows_ready, 1)

            def best_two(f, step):
                dve.wait_ge(scratch_filled, step + 1)
                nc.vector.tensor_copy(logits[:], scratch[0:SQ, 0:E]).then_inc(scratch_emptied, 1)
                dve.wait_ge(scratch_emptied, step + 1)
                alone(dve, dve_passed)
                nc.vector.max(top8[:], logits[:]).then_inc(top_ready, 1)
                dve.wait_ge(top_ready, f + 1)
                alone(dve, dve_passed)
                nc.vector.max_index(top_at[:], top8[:], logits[:]).then_inc(top_at_ready, 1)
                nc.vector.tensor_tensor(gate_diff[:], top8[:, 1:2], top8[:, 0:1], ALU.subtract
                                        ).then_inc(gate_diff_ready, 1)

            def pick(f):
                dve.wait_ge(top_at_ready, f + 1)
                nc.vector.tensor_copy(top_atf[:], top_at[:, 0:TOP]).then_inc(top_atf_ready, 1)
                dve.wait_ge(top_atf_ready, f + 1)
                nc.vector.tensor_tensor(picks[:], expert_ids[:].unsqueeze(1).broadcast_to([SQ, TOP, E]),
                                        top_atf[:].unsqueeze(2).broadcast_to([SQ, TOP, E]), ALU.is_equal
                                        ).then_inc(picks_ready, 1)
                dve.wait_ge(picks_ready, f + 1)
                nc.vector.tensor_tensor(chosen[:], picks[:, 0, :], picks[:, 1, :], ALU.add).then_inc(chosen_ready, 1)

            def rank(f, step):
                dve.wait_ge(gate_exp_ready, f + 1)
                nc.vector.tensor_scalar(gate_sum[:], gate_exp[:], 1.0, None, ALU.add).then_inc(gate_sum_ready, 1)
                dve.wait_ge(scratch_filled, step + 1)
                nc.vector.tensor_tensor(place[:], scratch[0:SQ, 0:E], base[:], ALU.add).then_inc(place_ready, 1)
                dve.wait_ge(gate_sum_ready, f + 1)
                nc.vector.reciprocal(rows[:, 0, WEIGHT:WEIGHT + 1], gate_sum[:]).then_inc(weight_ready, 1)
                nc.vector.tensor_tensor(base[:], scratch[0:SQ, E:2 * E], base[:], ALU.add
                                        ).then_inc(scratch_emptied, 1)
                dve.wait_ge(place_ready, f + 1)
                nc.vector.tensor_tensor(place_of[:], picks[:], place[:].unsqueeze(1).broadcast_to([SQ, TOP, E]),
                                        ALU.mult).then_inc(place_of_ready, 1)
                dve.wait_ge(weight_ready, f + 1)
                nc.vector.tensor_tensor(rows[:, 1, WEIGHT:WEIGHT + 1], rows[:, 0, WEIGHT:WEIGHT + 1], gate_exp[:],
                                        ALU.mult).then_inc(weights_ready, 1)
                dve.wait_ge(place_of_ready, f + 1)
                nc.vector.tensor_reduce(row_at[:], place_of[:], AX.X, ALU.add).then_inc(row_at_ready, 1)
                dve.wait_ge(row_at_ready, f + 1)
                nc.vector.tensor_copy(row_atu[:], row_at[:]).then_inc(routes_ready, 1)

            def finish(name, f, step):
                if name == "heads":
                    heads(f, step)
                if name == "project":
                    project(f, step)
                if name == "gate":
                    best_two(f, step)
                if name == "rank":
                    rank(f, step)

            def attend(p, b):
                for c in range(CHUNKS):
                    if c == 2 and later(b):
                        take_sums(b - 1)
                    if c >= 1:
                        clip(b, c - 1)
                    elif later(b):
                        clip(b - 1, CHUNKS - 1)
                    name, k = planned(b, c)
                    if name == "value":
                        take_values(1 - p, k, scratch_step(b, c))
                    if c:
                        split(*planned(b, c - 1), b + 1, scratch_step(b, c - 1))
                    finish(name, b - 1, scratch_step(b, c))
                    if later(b):
                        if c == PROJECTED + 1:
                            norm_tokens(b - 1)
                        if c == GATED + 1:
                            pick(b - 1)

            attend(0, 0)
            attend(1, 1)
            with dve.Fori(1, B // 2 - 1) as i:
                attend(0, 2 * i)
                attend(1, 2 * i + 1)
            attend(0, B - 2)
            attend(1, B - 1)
            clip(B - 1, CHUNKS - 1)
            take_sums(B - 1)
            for n, (name, k) in enumerate(FINISH):
                finish(name, B - 1, scratch_step(B - 1, CHUNKS) + n)
                if name == "project":
                    norm_tokens(B - 1)
                if name == "gate":
                    pick(B - 1)

            step = 0

            def chain(ins):
                nonlocal step
                step += 1
                ins.then_inc(table_step, 1)
                dve.wait_ge(table_step, step)

            dve.wait_ge(scratch_emptied, scratch_step(B - 1, CHUNKS) + len(FINISH))
            chain(nc.vector.scalar_tensor_tensor(out=tiles_i[:], in0=base[0:1, :], scalar=float(P - 1),
                                                 in1=first_row[:], op0=ALU.add, op1=ALU.subtract))
            chain(nc.vector.tensor_scalar(tiles_s[:], tiles_i[:], int(math.log2(P)), None, ALU.arith_shift_right))
            chain(nc.vector.tensor_copy(tiles_of[:], tiles_s[:]))
            src = tiles_of
            for n, shift in enumerate((1, 2, 4)):
                dst = ends[n % 2]
                nc.vector.tensor_copy(dst[:, 0:shift], src[:, 0:shift]).then_inc(table_step, 1)
                step += 1
                chain(nc.vector.tensor_tensor(dst[:, shift:E], src[:, shift:E], src[:, 0:E - shift], ALU.add))
                src = dst
            chain(nc.vector.tensor_tensor(passed, src[:].unsqueeze(1).broadcast_to([1, NT, E]),
                                          tile_no[:].unsqueeze(2).broadcast_to([1, NT, E]), ALU.is_le))
            nc.vector.tensor_reduce(tile_passed[:], passed, AX.X, ALU.add).then_inc(table_step, 1)
            step += 1
            chain(nc.vector.tensor_tensor(passed_tiles, passed,
                                          tiles_of[:].unsqueeze(1).broadcast_to([1, NT, E]), ALU.mult))
            nc.vector.tensor_scalar(table[:, 0, :], tile_passed[:], float(E - 1), None, ALU.min).then_inc(table_step, 1)
            step += 1
            chain(nc.vector.tensor_reduce(tile_start[:], passed_tiles, AX.X, ALU.add))
            chain(nc.vector.tensor_tensor(tile_shift[:], tile_no[:], tile_start[:], ALU.subtract))
            chain(nc.vector.tensor_scalar(tile_row[:], tile_passed[:], float(CAP // P), None, ALU.mult))
            chain(nc.vector.tensor_tensor(tile_shift[:], tile_row[:], tile_shift[:], ALU.add))
            nc.vector.tensor_scalar(table[:, 1, :], tile_shift[:], float(P), float(E * CAP), ALU.mult, ALU.min
                                    ).then_inc(table_ready, 1)
            dve.wait_ge(table_ready, 1)
            dve.wait_ge(w_experts_loaded, 16 * (1 + E))

            def place_w1(t, n):
                expert = dve.value_load(table[0:1, 0, bass.ds(t, 1)], min_val=0, max_val=E - 1)
                if not isinstance(t, int) or t >= 2:
                    dve.wait_ge(hidden_in_psum, t - 1)
                nc.vector.tensor_copy(w1_tile[:, n % 2, :], w1_sb[:, bass.ds(expert, 1), :].rearrange("p o f -> p (o f)")
                                      ).then_inc(w1_ready, 1)

            def take_home(t, n, i):
                dve.wait_ge(tile_loaded[n], 16 * (i + 1))
                if not isinstance(t, int) or t >= NB:
                    dve.wait_ge(y_sent[n], 16 * i)
                nc.vector.tensor_copy(tile_home[n][:], tile_in[n][:, HOME:HOME + 1]).then_inc(home_ready, 1)

            def weigh(t, n):
                dve.wait_ge(y_in_psum, t + 1)
                nc.vector.tensor_scalar(tile_out[n], scores[:, n % 2, 1, 0:D], tile_in[n][:, WEIGHT:WEIGHT + 1],
                                        None, ALU.mult).then_inc(y_ready, 1)

            place_w1(0, 0)

            def tile(t, n, i):
                if not (isinstance(t, int) and t == NT - 1):
                    place_w1(t + 1, n + 1)
                take_home(t, n, i)
                if not (isinstance(t, int) and t == 0):
                    weigh(t - 1, (n - 1) % NB)

            for n in range(NB):
                tile(n, n, 0)
            with dve.Fori(1, NT // NB) as i:
                for n in range(NB):
                    tile(NB * i + n, n, i)
            tile(NT - 1, 0, NT // NB)
            weigh(NT - 1, 0)

            for c in range(YCHUNKS):
                cols = slice(c * YB, (c + 1) * YB)
                dve.wait_ge(y_loaded[c], 16 * TOP)
                nc.vector.tensor_tensor(x_all[:, cols, :], x_all[:, cols, :], y_all[0][:, cols, :], ALU.add
                                        ).then_inc(y_step, 1)
                dve.wait_ge(y_step, c + 1)
                nc.vector.tensor_tensor(x_all[:, cols, :], x_all[:, cols, :], y_all[1][:, cols, :], ALU.add
                                        ).then_inc(out_ready, 1)


_INS = ['x', 'ctx_1024', 'mask_BxS_bf1', 'L0_xattn_W_q', 'L0_xattn_W_k', 'L0_xattn_W_v', 'L0_xattn_W_o',
        'L0_ffn_gate_w', 'L0_ffn_w1', 'L0_ffn_w2']
_OUTS = [((32, 100, 128), 'float32')]


def kernel(**inputs):
    import numpy as _np
    import concourse.bacc as _bacc
    from concourse import mybir as _mybir
    from concourse.bass_utils import run_bass_kernel_spmd as _run

    nc = _bacc.Bacc("TRN2", target_bir_lowering=False, num_devices=1)
    arrays, args = {}, []
    for name in _INS:
        a = _np.ascontiguousarray(inputs[name])
        if a.dtype == _np.bool_:
            a = a.view(_np.uint8)
        arrays[f"in_{name}_dram"] = a
        args.append(nc.dram_tensor(f"in_{name}_dram", a.shape, _mybir.dt.from_np(a.dtype), kind="ExternalInput").ap())
    for i, (shape, dtype) in enumerate(_OUTS):
        dt = _mybir.dt.from_np(_np.dtype(dtype))
        args.append(nc.dram_tensor(f"out_{i}_dram", shape, dt, kind="ExternalOutput").ap())
    xattn_moe(nc, *args)
    r = _run(nc, [arrays], core_ids=[0])
    got = tuple(r.results[0][f"out_{i}_dram"] for i in range(len(_OUTS)))
    return got[0]
```

```python
from contextlib import ExitStack
import math

import numpy as np
import concourse.bass as bass
from concourse import mybir

F32 = mybir.dt.float32
F32R = mybir.dt.float32r
U8 = mybir.dt.uint8
U32 = mybir.dt.uint32
I32 = mybir.dt.int32
ALU = mybir.AluOpType
ACT = mybir.ActivationFunctionType
AX = mybir.AxisListType

P = 128
HEADS = 16
EPS = 1e-5
CLIP = 50.0
TOP = 2


def xattn_moe(nc, x, ctx, mask, W_q, W_k, W_v, W_o, gate_w, w1, w2, out):
    B, SQ, D = x.shape
    SK = ctx.shape[1]
    E, _, F = w1.shape
    DH = D // HEADS
    TILES = -(-SK // P)
    FULL = SK // P
    TAIL = SK - FULL * P
    GROUPS = 4
    HG = HEADS // GROUPS
    GQ = HG * SQ
    PAIRS = HEADS // 2
    VW = 2 * DH + 1
    PQ = 2 * SQ
    CB = 3
    CHUNKS = TILES * GROUPS // CB
    RING = 8
    LAST_CHUNK = [(t * GROUPS + GROUPS - 1) // CB for t in range(TILES)]
    HALVES = 2 * TILES
    LAG = 2
    HALF_AT = [4 * (h // 6) + LAG + (1, 2, 2, 3, 4, 4)[h % 6] for h in range(HALVES)]
    KC = 4
    KSTEPS = TILES // KC
    KEY_COLS = [slice(k * KC * P, min((k + 1) * KC * P, SK)) for k in range(KSTEPS)]
    KEYS = [cols.stop - cols.start for cols in KEY_COLS]
    SCALE = 1.0 / math.sqrt(DH)
    LOW, HIGH = float(np.exp(np.float32(-CLIP))), float(np.exp(np.float32(CLIP)))
    KD = 16 * 4 * GROUPS
    QB = 4
    NQ = QB * SQ
    QSTEPS = B // QB
    DVE_NORMS = 4
    FC = F // P
    CAP = B * SQ
    ROW = D + 2
    TOKEN, HOME, WEIGHT = 0, D, D + 1
    NB = 8
    YCHUNKS = 8
    YB = B // YCHUNKS
    YPOOL = YB // 4
    NOWHERE = 1 << 20
    NT = (TOP * B * SQ + E * (P - 1)) // P
    assert (NT - 1) % NB == 0 and CAP % P == 0
    assert CHUNKS == 16 and TILES == 12 and B % 2 == 0 and D == P

    PREPARE = [("query", 0)]
    for k in range(KSTEPS):
        PREPARE += [("turn", k), ("key", k)]
    PREPARE += [("value", k) for k in range(KSTEPS)]
    FINISH = [("heads", 0), ("queries", 0), ("project", 0), ("tokens", 0), ("gate", 0), ("rank", 0)]
    STEPS = (PREPARE[1:7] + FINISH[:3] + PREPARE[:1] + PREPARE[7:8] + FINISH[3:5] + PREPARE[8:] + FINISH[5:])
    IN_LAST = [s in FINISH for s in STEPS]
    ALONE = PREPARE[7:9] + PREPARE[:1] + PREPARE[9:]
    FIRST_STEPS = [s if s in PREPARE else ("norm", QSTEPS - len(FINISH) + FINISH.index(s)) for s in STEPS]
    assert len(STEPS) == CHUNKS and QSTEPS - len(FINISH) == 2
    PROJECTED, GATED = STEPS.index(("project", 0)), STEPS.index(("gate", 0))

    def scratch_step(b, c):
        if isinstance(b, int) and b == B - 1:
            c = sum(IN_LAST[:c])
        return len(STEPS) * b + len(ALONE) + c

    def planned(b, c):
        if isinstance(b, int) and b == 0:
            return FIRST_STEPS[c]
        if isinstance(b, int) and b == B - 1 and not IN_LAST[c]:
            return None, 0
        return STEPS[c]

    def last_tile(c):
        return (c * CB + CB - 1) // GROUPS

    def later(b, least=1):
        return not isinstance(b, int) or b >= least

    def carry_wait(engine, told):
        engine.sem_inc(told, 1)

    es = ExitStack()
    with es:
        def sb(name, shape, dt=F32):
            return es.enter_context(nc.sbuf_tensor(name, shape, dt))

        def ps(name, shape):
            return es.enter_context(nc.psum_tensor(name, shape, F32))

        def sem(name):
            return es.enter_context(nc.semaphore(name))

        ident = sb("ident", [P, P])
        x_all = sb("x_all", [SQ, B, D])
        moments = sb("moments", [SQ, B, 2])
        rstd = sb("rstd", [SQ, B])
        half = sb("half", [SQ, B])
        mask_u8 = sb("mask_u8", [B, SQ], U8)
        mask_rows = sb("mask_rows", [B, SQ])
        mask_f = sb("mask_f", [SQ, B])
        w_turned = sb("w_turned", [P, 4, P])
        wq_rep = sb("wq_rep", [P, GROUPS, 4, HG * DH])
        q_parts = sb("q_parts", [P, GROUPS, SQ], F32R)
        own_head = sb("own_head", [P, 4, HG])
        head_mask = sb("head_mask", [P, HG])
        q_stack = [sb(f"q_stack{p}", [P, GROUPS, HG, SQ], F32R) for p in range(2)]
        xT_and_ctx = sb("xT_and_ctx", [P, B * SQ + TILES * D])
        xT = xT_and_ctx[:, 0:B * SQ]
        ctx_nat = [xT_and_ctx[:, B * SQ:].rearrange("p (t d) -> p t d", d=D),
                   sb("ctx_nat1", [P, TILES, D])[:]]
        w1_sb = xT_and_ctx[:, 0:E * F].rearrange("p (e f) -> p e f", e=E)
        ctxT = sb("ctxT", [P, TILES * P])
        k_full = sb("k_full", [P, KSTEPS, KC * P])
        q_full = sb("q_full", [P, GROUPS * SQ])
        k_hi = sb("k_hi", [P, TILES * P], F32R)
        k_lo = sb("k_lo", [P, TILES * P], F32R)
        k_stack = [sb(f"k_stack{p}", [P, GROUPS, TILES * P], F32R) for p in range(2)]
        v_both = sb("v_both", [P, 2, TILES, PAIRS, VW])
        v_ones = [v_both[:, p, :, :, :] for p in range(2)]
        probs = sb("probs", [P, RING, CB, GQ])
        first_normed = probs[0:SQ, 0, :, :].rearrange("q m c -> q (m c)")[:, 0:2 * QB * D].rearrange(
            "q (n j d) -> q n j d", n=2, j=QB)
        w_nat = probs[:, 1, :, :].rearrange("p m c -> p (m c)")[:, 0:4 * P].rearrange("p (n c) -> p n c", n=4)
        o_raw = sb("o_raw", [P, GQ])
        rden = sb("rden", [SQ, 4, GROUPS])
        attn = sb("attn", [SQ, D])
        attnT = sb("attnT", [P, SQ])
        stats1 = sb("stats1", [SQ, 6])
        moments1 = sb("moments1", [SQ, 2])
        rstd1 = sb("rstd1", [SQ, 2])
        rows = sb("rows", [SQ, TOP, ROW])
        zT = sb("zT", [P, SQ])
        gate_sb = sb("gate_sb", [P, E])
        logits = sb("logits", [SQ, E])
        top8 = sb("top8", [SQ, 8])
        top_at = sb("top_at", [SQ, 8], U32)
        top_atf = sb("top_atf", [SQ, TOP])
        expert_ids = sb("expert_ids", [SQ, E])
        expert_ids_i = sb("expert_ids_i", [SQ, E], I32)
        gate_diff = sb("gate_diff", [SQ, 1])
        gate_exp = sb("gate_exp", [SQ, 1])
        gate_sum = sb("gate_sum", [SQ, 1])
        warm = sb("warm", [SQ, 1])
        picks = sb("picks", [SQ, TOP, E])
        chosen = sb("chosen", [SQ, E])
        place = sb("place", [SQ, E])
        place_of = sb("place_of", [SQ, TOP, E])
        row_at = sb("row_at", [SQ, TOP])
        row_atu = sb("row_atu", [SQ, TOP], U32)
        base_i = sb("base_i", [SQ, E], I32)
        base = sb("base", [SQ, E])
        before = sb("before", [SQ, SQ])
        ones = sb("ones", [SQ, SQ])
        home_i = sb("home_i", [SQ, TOP], I32)
        home = sb("home", [SQ, TOP])
        fill = sb("fill", [P, ROW])
        w2_sb = sb("w2_sb", [P, E, FC, D])
        early = w2_sb[0:SQ, :, :, :].rearrange("q e c d -> q (e c d)")
        stats = early[:, 0:B * 6].rearrange("q (b s) -> q b s", b=B)
        later_normed = early[:, B * 6:B * 6 + (QSTEPS - 2) * QB * D].rearrange("q (n j d) -> q n j d", j=QB, d=D)
        normed = [first_normed[:, r, :, :] for r in range(2)] + [later_normed[:, r, :, :] for r in range(QSTEPS - 2)]
        first_row = sb("first_row", [1, E])
        tile_i = sb("tile_i", [1, NT], I32)
        tile_no = sb("tile_no", [1, NT])
        tiles_i = sb("tiles_i", [1, E], I32)
        tiles_s = sb("tiles_s", [1, E], I32)
        tiles_of = sb("tiles_of", [1, E])
        ends = [sb(f"ends{n}", [1, E]) for n in range(2)]
        nat1 = ctx_nat[1].rearrange("p t d -> p (t d)")
        passed, passed_unused = [nat1[0:1, n * NT * E:(n + 1) * NT * E].rearrange("q (t e) -> q t e", e=E)
                                 for n in range(2)]
        tile_passed, tile_skipped, tile_row = [o_raw[0:1, n * NT:(n + 1) * NT] for n in range(3)]
        unused = sb("unused", [1, E])
        table = sb("table", [1, 2, NT], I32)
        values = v_ones[0].rearrange("p t n w -> p (t n w)")
        tile_in = [values[:, n * ROW:(n + 1) * ROW] for n in range(NB)]
        tile_out = [ctx_nat[1][:, n, :] for n in range(NB)]
        tile_home = [sb(f"tile_home{n}", [P, 1], U32) for n in range(NB)]
        w1_tile = ctxT[:, 0:2 * F].rearrange("p (n f) -> p n f", n=2)
        tileT = ctxT[:, 2 * F:2 * F + 2 * P].rearrange("p (n r) -> p n r", n=2)
        hiddenT = k_full[:, 0:2, :].rearrange("p n (c r) -> p n c r", c=FC)
        y_all = [probs[0:SQ].rearrange("p r m q -> p (r m q)")[:, 0:B * D].rearrange("q (b d) -> q b d", b=B),
                 xT_and_ctx[0:SQ, 0:E * F].rearrange("q (b d) -> q b d", b=B)]
        expert_rows = nc.dram_tensor("expert_rows", [E * CAP + P, ROW], F32, kind="Internal").ap()
        outputs = nc.dram_tensor("expert_outputs", [TOP * B * SQ, D], F32, kind="Internal").ap()

        scores = ps("scores", [P, 2, CB, 512])
        o_sum = ps("o_sum", [P, 512])
        scratch = ps("scratch", [P, 512])

        x_loaded = [sem(f"x_loaded{h}") for h in range(2)]
        w_loaded = sem("w_loaded")
        mask_loaded = sem("mask_loaded")
        ctx_turned = sem("ctx_turned")
        ctxT_ready = sem("ctxT_ready")
        keys_projected = sem("keys_projected")
        mask_cast = sem("mask_cast")
        mask_in_psum = sem("mask_in_psum")
        mask_ready = sem("mask_ready")
        cleared = sem("cleared")
        ident_ready = sem("ident_ready")
        o_cleared = sem("o_cleared")
        stats_ready = sem("stats_ready")
        moments_ready = sem("moments_ready")
        var_ready = sem("var_ready")
        half_ready = sem("half_ready")
        rstd_ready = sem("rstd_ready")
        normed_ready = sem("normed_ready")
        w_in_psum = sem("w_in_psum")
        w_turned_ready = sem("w_turned_ready")
        xT_in_psum = sem("xT_in_psum")
        xT_ready = sem("xT_ready")
        wq_rep_ready = sem("wq_rep_ready")
        own_head_step = sem("own_head_step")
        head_mask_ready = sem("head_mask_ready")
        q_hi_ready = sem("q_hi_ready")
        q_stacked = sem("q_stacked")
        ctx_loaded = [sem(f"ctx_loaded{p}") for p in range(2)]
        scratch_filled = sem("scratch_filled")
        scratch_emptied = sem("scratch_emptied")
        k_hi_ready = sem("k_hi_ready")
        k_split = sem("k_split")
        q_split = sem("q_split")
        k_stacked = sem("k_stacked")
        scores_ready = sem("scores_ready")
        exp_ready = sem("exp_ready")
        probs_ready = sem("probs_ready")
        pv_done = sem("pv_done")
        o_taken = sem("o_taken")
        rden_ready = sem("rden_ready")
        stats1_ready = sem("stats1_ready")
        moments1_ready = sem("moments1_ready")
        var1_ready = sem("var1_ready")
        rstd1_ready = sem("rstd1_ready")
        rows_ready = sem("rows_ready")
        gate_loaded = sem("gate_loaded")
        top_ready = sem("top_ready")
        top_at_ready = sem("top_at_ready")
        top_atf_ready = sem("top_atf_ready")
        gate_diff_ready = sem("gate_diff_ready")
        gate_exp_ready = sem("gate_exp_ready")
        gate_sum_ready = sem("gate_sum_ready")
        weight_ready = sem("weight_ready")
        weights_ready = sem("weights_ready")
        picks_ready = sem("picks_ready")
        chosen_ready = sem("chosen_ready")
        place_ready = sem("place_ready")
        place_of_ready = sem("place_of_ready")
        row_at_ready = sem("row_at_ready")
        routes_ready = sem("routes_ready")
        homes_written = sem("homes_written")
        homes_next = sem("homes_next")
        before_step = sem("before_step")
        ones_ready = sem("ones_ready")
        ids_step = sem("ids_step")
        fill_step = sem("fill_step")
        rows_filled = sem("rows_filled")
        spare_rows_filled = sem("spare_rows_filled")
        rows_sent = sem("rows_sent")
        w_experts_loaded = sem("w_experts_loaded")
        table_step = sem("table_step")
        table_ready = sem("table_ready")
        tile_turned = sem("tile_turned")
        tileT_ready = sem("tileT_ready")
        w1_ready = sem("w1_ready")
        hidden_in_psum = sem("hidden_in_psum")
        hidden_ready = sem("hidden_ready")
        y_in_psum = sem("y_in_psum")
        home_ready = sem("home_ready")
        y_ready = sem("y_ready")
        y_step = sem("y_step")
        out_ready = sem("out_ready")
        y_step_pool = sem("y_step_pool")
        out_ready_pool = sem("out_ready_pool")
        out_stored = sem("out_stored")
        tile_loaded = [sem(f"tile_loaded{n}") for n in range(NB)]
        y_sent = [sem(f"y_sent{n}") for n in range(NB)]
        y_loaded = [sem(f"y_loaded{n}") for n in range(YCHUNKS)]

        dve_passed = sem("dve_passed")
        pool_passed = sem("pool_passed")
        sp_passed = sem("sp_passed")

        WQ, WK, WV, WO = range(4)

        def add_outputs(engine, arithmetic, start, stop, first_added, both_added):
            for c in range(YCHUNKS):
                cols = slice(c * YB + start, c * YB + stop)
                engine.wait_ge(y_loaded[c], 16 * TOP)
                arithmetic.tensor_tensor(x_all[:, cols, :], x_all[:, cols, :], y_all[0][:, cols, :], ALU.add
                                         ).then_inc(first_added, 1)
                engine.wait_ge(first_added, c + 1)
                arithmetic.tensor_tensor(x_all[:, cols, :], x_all[:, cols, :], y_all[1][:, cols, :], ALU.add
                                         ).then_inc(both_added, 1)

        block = es.enter_context(nc.Block())

        @block.sync
        def _(sp):
            def load_ctx(b, p):
                sp.dma_start(ctx_nat[p][:, 0:FULL, :],
                             ctx[b, 0:FULL * P, :].rearrange("(p t) d -> p t d", t=FULL)
                             ).then_inc(ctx_loaded[p], 16)
                sp.dma_start(ctx_nat[p][0:TAIL, FULL, :], ctx[b, FULL * P:SK, :]
                             ).then_inc(ctx_loaded[p], 16)

            for n, w in enumerate((W_q, W_k, W_v, W_o)):
                sp.dma_start(w_nat[:, n, :], w).then_inc(w_loaded, 16)
            load_ctx(0, 0)
            sp.dma_start(mask_u8[:], mask).then_inc(mask_loaded, 16)
            for h in range(2):
                part = slice(0, QB) if h == 0 else slice(QB, B)
                sp.dma_start(x_all[:, part, :], x[part].rearrange("b q d -> q b d")).then_inc(x_loaded[h], 16)
            load_ctx(1, 1)
            sp.dma_start(gate_sb[:], gate_w).then_inc(gate_loaded, 16)

            def fill_rows(b):
                if later(b):
                    sp.wait_ge(rows_filled, 16 * b)
                sp.dma_start(expert_rows[0:E * CAP, :].rearrange("(e r) c -> r e c", e=E)[bass.ds(b * SQ, SQ)],
                             fill[0:SQ, :].unsqueeze(1).broadcast_to([SQ, E, ROW])).then_inc(rows_filled, 16)

            def stack_keys(p):
                R = HG * DH
                for t, part in enumerate((k_hi, k_lo, k_hi, k_lo)):
                    for g in range(GROUPS):
                        sp.dma_start(k_stack[p][t * R:(t + 1) * R, g, :].bitcast(F32),
                                     part[g * R:(g + 1) * R, :].bitcast(F32)).then_inc(k_stacked, 16)

            sp.wait_ge(cleared, 3)
            sp.wait_ge(k_split, KSTEPS)
            stack_keys(0)
            sp.wait_ge(fill_step, 2)
            sp.dma_start(expert_rows[E * CAP:E * CAP + P, :], fill[:]).then_inc(spare_rows_filled, 16)
            fill_rows(0)

            def during(b, p):
                if later(b):
                    sp.wait_ge(scores_ready, CHUNKS * b)
                    carry_wait(sp, sp_passed)
                if not (isinstance(b, int) and b + 2 >= B):
                    sp.wait_ge(scratch_filled, scratch_step(b, 0))
                    load_ctx(b + 2, p)
                fill_rows(b + 1)
                sp.wait_ge(k_split, KSTEPS * (b + 2))
                stack_keys(1 - p)

            during(0, 0)
            during(1, 1)
            with sp.Fori(1, B // 2 - 1) as i:
                during(2 * i, 0)
                during(2 * i + 1, 1)
            during(B - 2, 0)
            sp.wait_ge(scratch_filled, scratch_step(B - 2, STEPS.index(("query", 0))) + 1)
            sp.dma_start(w1_sb, w1.rearrange("e d f -> d e f")).then_inc(w_experts_loaded, 16)
            for e in range(E):
                sp.dma_start(w2_sb[:, e, :, :], w2[e].rearrange("(c f) d -> f c d", f=P)
                             ).then_inc(w_experts_loaded, 16)

            sp.wait_ge(rows_sent, 16 * TOP * B)
            sp.wait_ge(spare_rows_filled, 16)
            sp.wait_ge(table_ready, 1)

            def load_tile(t, n):
                if not isinstance(t, int) or t >= NB:
                    sp.wait_ge(y_ready, t - NB + 1)
                row = sp.value_load(table[0:1, 1, bass.ds(t, 1)], min_val=0, max_val=E * CAP)
                sp.dma_start(tile_in[n], expert_rows[bass.ds(row, P), :]).then_inc(tile_loaded[n], 16)

            for t in range(NB):
                load_tile(t, t)
            with sp.Fori(1, NT // NB) as i:
                for n in range(NB):
                    load_tile(NB * i + n, n)
            load_tile(NT - 1, 0)

            for n in range(NB):
                sp.wait_ge(y_sent[n], 16 * (NT // NB + (n == 0)))
            for c in range(YCHUNKS):
                for k in range(TOP):
                    first_row_of = (k * B + c * YB) * SQ
                    sp.dma_start(y_all[k][:, c * YB:(c + 1) * YB, :],
                                 outputs[first_row_of:first_row_of + YB * SQ, :].rearrange("(b q) d -> q b d", q=SQ)
                                 ).then_inc(y_loaded[c], 16)
            for c in range(YCHUNKS):
                sp.wait_ge(out_ready, c + 1)
                sp.wait_ge(out_ready_pool, c + 1)
                sp.dma_start(out[c * YB:(c + 1) * YB].rearrange("b q d -> q b d"),
                             x_all[:, c * YB:(c + 1) * YB, :]).then_inc(out_stored, 16)
            sp.wait_ge(out_stored, 16 * YCHUNKS)

        @block.gpsimd
        def _(pool):
            for padded in (ctxT[:], k_hi[:].bitcast(F32), k_lo[:].bitcast(F32)):
                nc.gpsimd.memset(padded[:, SK:TILES * P], 0.0).then_inc(cleared, 1)
            nc.gpsimd.memset(half[:], -0.5).then_inc(half_ready, 1)
            for p in range(2):
                nc.gpsimd.memset(v_ones[p][:, 0:FULL, :, 2 * DH], 1.0).then_inc(cleared, 1)
                nc.gpsimd.memset(v_ones[p][:, FULL, :, 2 * DH], 0.0).then_inc(cleared, 1)
            pool.wait_ge(cleared, 7)
            for p in range(2):
                nc.gpsimd.memset(v_ones[p][0:TAIL, FULL, :, 2 * DH], 1.0).then_inc(cleared, 1)
            nc.gpsimd.memset(ident[:], 0.0).then_inc(ident_ready, 1)
            pool.wait_ge(ident_ready, 1)
            nc.gpsimd.affine_select(out=ident[:], in_=ident[:], compare_op=ALU.not_equal, fill=1.0,
                                    base=0, pattern=[[-1, P]], channel_multiplier=1).then_inc(ident_ready, 1)
            nc.gpsimd.memset(own_head[:], 1.0).then_inc(own_head_step, 1)
            pool.wait_ge(own_head_step, 1)
            nc.gpsimd.affine_select(out=own_head[:], in_=own_head[:], compare_op=ALU.is_ge, fill=0.0, base=0,
                                    pattern=[[-HG * DH, 4], [-DH, HG]], channel_multiplier=1
                                    ).then_inc(own_head_step, 1)
            pool.wait_ge(own_head_step, 2)
            nc.gpsimd.affine_select(out=own_head[:], in_=own_head[:], compare_op=ALU.is_ge, fill=0.0, base=DH - 1,
                                    pattern=[[HG * DH, 4], [DH, HG]], channel_multiplier=-1
                                    ).then_inc(own_head_step, 1)
            def stack_queries(p, b):
                pool.wait_ge(q_split, b + 1)
                if later(b, 2):
                    pool.wait_ge(scores_ready, CHUNKS * (b - 1))
                nc.gpsimd.tensor_tensor(
                    q_stack[p][:], q_parts[:].bitcast(F32).unsqueeze(2).broadcast_to([P, GROUPS, HG, SQ]),
                    head_mask[:].unsqueeze(1).unsqueeze(3).broadcast_to([P, GROUPS, HG, SQ]), ALU.mult
                ).then_inc(q_stacked, 1)

            pool.wait_ge(half_ready, 1)
            def invert_deviations(r):
                part = slice(r * QB, (r + 1) * QB)
                pool.wait_ge(moments_ready, r + 1)
                nc.gpsimd.tensor_scalar(rstd[:, part], moments[:, part, 1], EPS, None, ALU.add).then_inc(var_ready, 1)
                pool.wait_ge(var_ready, r + 1)
                nc.gpsimd.tensor_tensor(rstd[:, part], rstd[:, part], half[:, part], ALU.pow).then_inc(rstd_ready, 1)

            for r in range(2):
                invert_deviations(r)
            nc.gpsimd.memset(fill[:], 0.0).then_inc(fill_step, 1)
            pool.wait_ge(fill_step, 1)
            nc.gpsimd.memset(fill[:, HOME:HOME + 1], float(NOWHERE)).then_inc(fill_step, 1)
            nc.gpsimd.memset(before[:], 1.0).then_inc(before_step, 1)
            pool.wait_ge(before_step, 1)
            nc.gpsimd.affine_select(out=before[:], in_=before[:], compare_op=ALU.is_ge, fill=0.0, base=-1,
                                    pattern=[[1, SQ]], channel_multiplier=-1).then_inc(before_step, 1)
            nc.gpsimd.memset(ones[:], 1.0).then_inc(ones_ready, 1)
            nc.gpsimd.iota(expert_ids_i[:], pattern=[[1, E]], base=0, channel_multiplier=0).then_inc(ids_step, 1)
            nc.gpsimd.iota(base_i[:], pattern=[[CAP, E]], base=0, channel_multiplier=0).then_inc(ids_step, 1)
            nc.gpsimd.iota(home_i[:], pattern=[[B * SQ, TOP]], base=0, channel_multiplier=1).then_inc(ids_step, 1)
            nc.gpsimd.iota(tile_i[:], pattern=[[1, NT]], base=0, channel_multiplier=0).then_inc(ids_step, 1)
            for r in range(2, DVE_NORMS):
                invert_deviations(r)
            pool.wait_ge(head_mask_ready, 1)
            stack_queries(0, 0)
            for r in range(DVE_NORMS, QSTEPS):
                invert_deviations(r)
                pool.wait_ge(rstd_ready, r + 1)
                for j in range(QB):
                    b = r * QB + j
                    nc.gpsimd.tensor_scalar(normed[r][:, j, :], x_all[:, b, :], moments[:, b, 0:1],
                                            rstd[:, b:b + 1], ALU.subtract, ALU.mult).then_inc(normed_ready, 1)

            def invert_deviation(f):
                pool.wait_ge(homes_next, f + 1)
                if later(f):
                    pool.wait_ge(rows_sent, 16 * TOP * f)
                carry_wait(pool, pool_passed)
                nc.gpsimd.tensor_copy(rows[:, :, HOME], home[:]).then_inc(homes_written, 1)
                pool.wait_ge(homes_written, f + 1)
                carry_wait(pool, pool_passed)
                nc.gpsimd.tensor_scalar(home[:], home[:], float(SQ), None, ALU.add).then_inc(homes_next, 1)
                pool.wait_ge(moments1_ready, f + 1)
                carry_wait(pool, pool_passed)
                nc.gpsimd.tensor_scalar(rstd1[:, 0:1], moments1[:, 1:2], EPS, None, ALU.add).then_inc(var1_ready, 1)
                pool.wait_ge(var1_ready, f + 1)
                nc.gpsimd.tensor_tensor(rstd1[:, 1:2], rstd1[:, 0:1], half[:, 0:1], ALU.pow).then_inc(rstd1_ready, 1)

            def route(f):
                pool.wait_ge(routes_ready, f + 1)
                pool.wait_ge(rows_filled, 16 * (f + 1))
                carry_wait(pool, pool_passed)
                for k in range(TOP):
                    nc.gpsimd.indirect_dma_start(
                        out=expert_rows[0:E * CAP, :], out_offset=bass.IndirectOffsetOnAxis(ap=row_atu[:, k:k + 1], axis=0),
                        in_=rows[:, k, :], in_offset=None).then_inc(rows_sent, 16)

            def during(b, p):
                if later(b):
                    invert_deviation(b - 1)
                if not (isinstance(b, int) and b == B - 1):
                    stack_queries(1 - p, b + 1)
                if later(b):
                    route(b - 1)

            during(0, 0)
            during(1, 1)
            with pool.Fori(1, B // 2 - 1) as i:
                during(2 * i, 0)
                during(2 * i + 1, 1)
            during(B - 2, 0)
            during(B - 1, 1)
            invert_deviation(B - 1)
            route(B - 1)

            def send(t, n):
                pool.wait_ge(y_ready, t + 1)
                carry_wait(pool, pool_passed)
                nc.gpsimd.indirect_dma_start(
                    out=outputs[:, :], out_offset=bass.IndirectOffsetOnAxis(ap=tile_home[n][:], axis=0),
                    in_=tile_out[n], in_offset=None, bounds_check=TOP * B * SQ - 1, oob_is_err=False
                ).then_inc(y_sent[n], 16)

            with pool.Fori(0, NT // NB) as i:
                for n in range(NB):
                    send(NB * i + n, n)
            send(NT - 1, 0)
            add_outputs(pool, nc.gpsimd, YB - YPOOL, YB, y_step_pool, out_ready_pool)

        @block.tensor
        def _(pe):
            def turn_ctx(into, p, k):
                for j in range(KC):
                    n = P if k * KC + j < FULL else TAIL
                    last = nc.tensor.transpose(into[:, j * P:j * P + n], ctx_nat[p][0:n, k * KC + j, :],
                                               ident[0:n, 0:n])
                return last

            def project_k(into, k):
                return nc.tensor.matmul(into[:, 0:KEYS[k]], w_turned[:, WK, :], ctxT[:, KEY_COLS[k]],
                                        start=True, stop=True)

            def project_q(b):
                cols = slice(b * SQ, (b + 1) * SQ) if isinstance(b, int) else bass.ds(b * SQ, SQ)
                for g in range(GROUPS):
                    last = nc.tensor.matmul(scratch[:, g * SQ:(g + 1) * SQ],
                                            wq_rep[:, g, :, :].rearrange("p t r -> p (t r)"),
                                            xT[:, cols], start=True, stop=True)
                return last

            def project_v(k):
                for j in range(KC):
                    t = k * KC + j
                    last = nc.tensor.matmul(scratch[:, j * P:(j + 1) * P], ctxT[:, t * P:(t + 1) * P],
                                            w_turned[:, WV, :], start=True, stop=True)
                return last

            def turn_tokens(into, r):
                pe.wait_ge(normed_ready, QB * (r + 1))
                for j in range(QB):
                    last = nc.tensor.transpose(into[:, j * SQ:(j + 1) * SQ], normed[r][:, j, :],
                                               ident[0:SQ, 0:SQ])
                return last

            def into_scratch(name, k, p, b, f, step):
                if not (isinstance(step, int) and step == 0):
                    pe.wait_ge(scratch_emptied, step)
                if name == "norm":
                    last = turn_tokens(scratch, k)
                elif name == "query":
                    last = project_q(b)
                elif name == "turn":
                    last = turn_ctx(scratch, p, k)
                elif name == "key":
                    last = project_k(scratch, k)
                elif name == "value":
                    last = project_v(k)
                elif name == "heads":
                    pe.wait_ge(o_taken, f + 1)
                    for n in range(4):
                        last = nc.tensor.transpose(scratch[0:SQ, n * P:(n + 1) * P],
                                                   o_raw[:, n * SQ:(n + 1) * SQ], ident[:])
                elif name == "queries":
                    last = nc.tensor.transpose(scratch[:, 0:SQ], attn[:], ident[0:SQ, 0:SQ])
                elif name == "project":
                    last = nc.tensor.matmul(scratch[0:SQ, 0:D], attnT[:], w_turned[:, WO, :],
                                            start=True, stop=True)
                elif name == "tokens":
                    pe.wait_ge(rows_ready, f + 1)
                    last = nc.tensor.transpose(scratch[:, 0:SQ], rows[:, 0, TOKEN:D], ident[0:SQ, 0:SQ])
                elif name == "gate":
                    if isinstance(f, int) and f == 0:
                        pe.wait_ge(gate_loaded, 16)
                    last = nc.tensor.matmul(scratch[0:SQ, 0:E], zT[:], gate_sb[:], start=True, stop=True)
                else:
                    pe.wait_ge(chosen_ready, f + 1)
                    if isinstance(f, int) and f == 0:
                        pe.wait_ge(before_step, 2)
                        pe.wait_ge(ones_ready, 1)
                    nc.tensor.matmul(scratch[0:SQ, 0:E], before[:], chosen[:], start=True, stop=True)
                    last = nc.tensor.matmul(scratch[0:SQ, E:2 * E], ones[:], chosen[:], start=True, stop=True)
                last.then_inc(scratch_filled, 1)

            def score_chunk(p, c):
                for m in range(CB):
                    t, g = divmod(c * CB + m, GROUPS)
                    last = nc.tensor.matmul(scores[:, c % 2, m, 0:GQ],
                                            k_stack[p][:, g, t * P:(t + 1) * P],
                                            q_stack[p][:, g, :, :].rearrange("p h q -> p (h q)"),
                                            start=True, stop=True)
                last.then_inc(scores_ready, 1)

            def weigh_values(p, h):
                t, s = divmod(h, 2)
                for g in range(GROUPS):
                    c, m = divmod(t * GROUPS + g, CB)
                    last = nc.tensor.matmul(o_sum[32 * g:32 * g + VW, s * PQ:(s + 1) * PQ],
                                            v_ones[p][:, t, 2 * g + s, :],
                                            probs[:, c % RING, m, s * PQ:(s + 1) * PQ],
                                            start=(t == 0 and s == 0), stop=(t == TILES - 1),
                                            skip_group_check=True)
                last.then_inc(pv_done, 1)

            pe.wait_ge(w_loaded, 64)
            pe.wait_ge(ident_ready, 2)
            for n in range(4):
                last = nc.tensor.transpose(scores[:, 1, 2, n * P:(n + 1) * P], w_nat[:, n, :], ident[:])
            last.then_inc(w_in_psum, 1)
            pe.wait_ge(ctx_loaded[0], 32)
            pe.wait_ge(cleared, 3)
            for k in range(KSTEPS):
                turn_ctx(scores[:, 0, k, :], 0, k).then_inc(ctx_turned, 1)
            pe.wait_ge(w_turned_ready, 1)
            for k in range(KSTEPS):
                pe.wait_ge(ctxT_ready, k + 1)
                project_k(scores[:, 1, k, :], k).then_inc(keys_projected, 1)
            pe.wait_ge(mask_cast, 1)
            nc.tensor.transpose(scores[0:SQ, 0, 2, 0:B], mask_rows[:], ident[0:B, 0:B]).then_inc(mask_in_psum, 1)
            for step, (name, k) in enumerate(ALONE):
                if name == "query":
                    for r in range(2):
                        turn_tokens(scores[:, 0, r, :], r).then_inc(xT_in_psum, 1)
                    pe.wait_ge(xT_ready, 1)
                    pe.wait_ge(wq_rep_ready, 1)
                into_scratch(name, k, 0, 0, None, step)
            pe.wait_ge(xT_ready, 2)
            pe.wait_ge(k_split, KSTEPS)
            pe.wait_ge(mask_ready, 1)
            pe.wait_ge(q_stacked, 1)
            pe.wait_ge(k_stacked, KD)
            score_chunk(0, 0)

            def attend(i, p, b, last_one):
                for c in range(CHUNKS):
                    if c + 1 < CHUNKS:
                        if later(b) or c >= 1:
                            pe.wait_ge(exp_ready, CHUNKS * b + c)
                        score_chunk(p, c + 1)
                    elif not last_one:
                        pe.wait_ge(q_stacked, b + 2)
                        pe.wait_ge(k_stacked, KD * (b + 2))
                        pe.wait_ge(exp_ready, CHUNKS * b + c)
                        score_chunk(1 - p, 0)
                    name, k = planned(b, c)
                    if name == "turn" and k == 0:
                        pe.wait_ge(ctx_loaded[1 - p], 32 * (i + 1 + p))
                    if name:
                        into_scratch(name, k, 1 - p, b + 1, b - 1, scratch_step(b, c))
                    for h in range(HALVES):
                        if HALF_AT[h] == c:
                            pe.wait_ge(probs_ready, CHUNKS * b + LAST_CHUNK[h // 2] + 1)
                            if h == 0 and later(b):
                                pe.wait_ge(o_taken, b)
                            elif h == 0:
                                pe.wait_ge(o_cleared, 1)
                                pe.wait_ge(cleared, 9)
                            weigh_values(p, h)
                        elif HALF_AT[h] == c + CHUNKS and later(b):
                            pe.wait_ge(probs_ready, CHUNKS * (b - 1) + LAST_CHUNK[h // 2] + 1)
                            weigh_values(1 - p, h)

            attend(0, 0, 0, False)
            attend(0, 1, 1, False)
            with pe.Fori(1, B // 2 - 1) as i:
                attend(i, 0, 2 * i, False)
                attend(i, 1, 2 * i + 1, False)
            attend(B // 2 - 1, 0, B - 2, False)
            attend(B // 2 - 1, 1, B - 1, True)
            for h in range(HALVES):
                if HALF_AT[h] >= CHUNKS:
                    pe.wait_ge(probs_ready, CHUNKS * (B - 1) + LAST_CHUNK[h // 2] + 1)
                    weigh_values(1, h)
            for n, (name, k) in enumerate(FINISH):
                into_scratch(name, k, None, None, B - 1, scratch_step(B - 1, CHUNKS) + n)

            pe.wait_ge(scratch_emptied, scratch_step(B - 1, CHUNKS) + len(FINISH))
            pe.wait_ge(table_ready, 2)
            pe.wait_ge(w_experts_loaded, 16 * (1 + E))

            def turn_tile(t, n, i):
                pe.wait_ge(tile_loaded[n], 16 * (i + 1))
                if not isinstance(t, int) or t >= 2:
                    pe.wait_ge(tileT_ready, t - 1)
                nc.tensor.transpose(scores[:, n % 2, 2, 0:P], tile_in[n][:, TOKEN:D], ident[:]
                                    ).then_inc(tile_turned, 1)

            def up(t, n):
                pe.wait_ge(tileT_ready, t + 1)
                pe.wait_ge(w1_ready, t + 1)
                if not isinstance(t, int) or t >= 2:
                    pe.wait_ge(hidden_ready, t - 1)
                for c in range(FC):
                    last = nc.tensor.matmul(scores[:, n % 2, 0, c * P:(c + 1) * P],
                                            w1_tile[:, n % 2, c * P:(c + 1) * P], tileT[:, n % 2, :],
                                            start=True, stop=True)
                last.then_inc(hidden_in_psum, 1)

            def down(t, n):
                expert = pe.value_load(table[0:1, 0, bass.ds(t, 1)], min_val=0, max_val=E - 1)
                pe.wait_ge(hidden_ready, t + 1)
                if not isinstance(t, int) or t >= 2:
                    pe.wait_ge(y_ready, t - 1)
                for c in range(FC):
                    last = nc.tensor.matmul(scores[:, n % 2, 1, 0:D], hiddenT[:, n % 2, c, :],
                                            w2_sb[:, bass.ds(expert, 1), c, :].rearrange("f o d -> f (o d)"),
                                            start=(c == 0), stop=(c == FC - 1))
                last.then_inc(y_in_psum, 1)

            turn_tile(0, 0, 0)

            def tile(t, n, i):
                if not (isinstance(t, int) and t == NT - 1):
                    turn_tile(t + 1, (n + 1) % NB, i + (n + 1) // NB)
                up(t, n)
                if not (isinstance(t, int) and t == 0):
                    down(t - 1, (n - 1) % NB)

            for n in range(NB):
                tile(n, n, 0)
            with pe.Fori(1, NT // NB) as i:
                for n in range(NB):
                    tile(NB * i + n, n, i)
            tile(NT - 1, 0, NT // NB)
            down(NT - 1, 0)

        @block.scalar
        def _(act):
            act.wait_ge(w_in_psum, 1)
            nc.scalar.copy(w_turned[:].rearrange("p n d -> p (n d)"), scores[:, 1, 2, :]
                           ).then_inc(w_turned_ready, 1)
            for k in range(KSTEPS):
                act.wait_ge(ctx_turned, k + 1)
                nc.scalar.copy(ctxT[:, KEY_COLS[k]], scores[:, 0, k, 0:KEYS[k]]).then_inc(ctxT_ready, 1)

            act.wait_ge(w_turned_ready, 1)
            nc.scalar.copy(wq_rep[:], w_turned[:, WQ, :].rearrange("p (g r) -> p g r", g=GROUPS)
                           .unsqueeze(2).broadcast_to([P, GROUPS, 4, HG * DH])).then_inc(wq_rep_ready, 1)

            def take(name, k, b, f, step):
                if name not in ("norm", "turn", "key", "query", "queries", "tokens"):
                    return
                act.wait_ge(scratch_filled, step + 1)
                if name == "norm":
                    nc.scalar.copy(xT[:, k * NQ:(k + 1) * NQ], scratch[:, 0:NQ]).then_inc(scratch_emptied, 1)
                elif name == "turn":
                    nc.scalar.copy(ctxT[:, KEY_COLS[k]], scratch[:, 0:KEYS[k]]).then_inc(scratch_emptied, 1)
                elif name == "key":
                    if later(b):
                        act.wait_ge(k_split, KSTEPS * (b - 1) + k + 1)
                    nc.scalar.copy(k_full[:, k, 0:KEYS[k]], scratch[:, 0:KEYS[k]]).then_inc(scratch_emptied, 1)
                elif name == "query":
                    if later(b):
                        act.wait_ge(q_split, b)
                    nc.scalar.copy(q_full[:], scratch[:, 0:GROUPS * SQ]).then_inc(scratch_emptied, 1)
                elif name == "queries":
                    nc.scalar.copy(attnT[:], scratch[:, 0:SQ]).then_inc(scratch_emptied, 1)
                else:
                    nc.scalar.copy(zT[:], scratch[:, 0:SQ]).then_inc(scratch_emptied, 1)

            def second_share(f):
                act.wait_ge(gate_diff_ready, f + 1)
                nc.scalar.activation(gate_exp[:], gate_diff[:], ACT.Exp).then_inc(gate_exp_ready, 1)

            for step, (name, k) in enumerate(ALONE):
                if name == "query":
                    for r in range(2):
                        act.wait_ge(xT_in_psum, r + 1)
                        nc.scalar.copy(xT[:, r * NQ:(r + 1) * NQ], scores[:, 0, r, 0:NQ]).then_inc(xT_ready, 1)
                if name == "value":
                    act.wait_ge(scratch_filled, step + 1)
                    nc.scalar.copy(v_ones[0][:, k * KC:(k + 1) * KC, :, 0:2 * DH],
                                   scratch[:].rearrange("p (t n d) -> p t n d", t=KC, n=PAIRS)
                                   ).then_inc(scratch_emptied, 1)
                take(name, k, 0, None, step)

            def attend(b):
                for c in range(CHUNKS):
                    act.wait_ge(scores_ready, CHUNKS * b + c + 1)
                    if later(b) or c >= RING:
                        act.wait_ge(pv_done, HALVES * b + 2 * last_tile(c - RING) + 2)
                    nc.scalar.activation(probs[:, c % RING, :, :], scores[:, c % 2, :, 0:GQ], ACT.Exp,
                                         scale=SCALE).then_inc(exp_ready, 1)
                    name, k = planned(b, c)
                    take(name, k, b + 1, b - 1, scratch_step(b, c))
                    if c == GATED + 2 and later(b):
                        second_share(b - 1)

            attend(0)
            attend(1)
            with act.Fori(1, B // 2 - 1) as i:
                attend(2 * i)
                attend(2 * i + 1)
            attend(B - 2)
            attend(B - 1)
            for n, (name, k) in enumerate(FINISH):
                take(name, k, None, B - 1, scratch_step(B - 1, CHUNKS) + n)
            second_share(B - 1)
            nc.scalar.activation(warm[:], gate_diff[:], ACT.Gelu_apprx_tanh)

            def take_tile(t, n):
                act.wait_ge(tile_turned, t + 1)
                if not isinstance(t, int) or t >= 2:
                    act.wait_ge(hidden_in_psum, t - 1)
                nc.scalar.copy(tileT[:, n % 2, :], scores[:, n % 2, 2, 0:P]).then_inc(tileT_ready, 1)

            def gelu(t, n):
                act.wait_ge(hidden_in_psum, t + 1)
                if not isinstance(t, int) or t >= 2:
                    act.wait_ge(y_in_psum, t - 1)
                nc.scalar.activation(hiddenT[:, n % 2, :, :], scores[:, n % 2, 0, :].rearrange("p (c r) -> p c r", c=FC),
                                     ACT.Gelu_apprx_tanh).then_inc(hidden_ready, 1)

            take_tile(0, 0)

            def tile(t, n):
                if not (isinstance(t, int) and t == NT - 1):
                    take_tile(t + 1, n + 1)
                gelu(t, n)

            for n in range(NB):
                tile(n, n)
            with act.Fori(1, NT // NB) as i:
                for n in range(NB):
                    tile(NB * i + n, n)
            tile(NT - 1, 0)

        @block.vector
        def _(dve):
            nc.vector.memset(o_sum[:], 0.0).then_inc(o_cleared, 1)
            def split_keys(b, k, step):
                cols = KEY_COLS[k]
                dve.wait_ge(scratch_emptied, step + 1)
                if later(b):
                    dve.wait_ge(k_stacked, KD * b)
                nc.vector.tensor_copy(k_hi[:, cols], k_full[:, k, 0:KEYS[k]]).then_inc(k_hi_ready, 1)
                dve.wait_ge(k_hi_ready, KSTEPS * b + k + 1)
                nc.vector.tensor_tensor(k_lo[:, cols], k_full[:, k, 0:KEYS[k]], k_hi[:, cols].bitcast(F32),
                                        ALU.subtract).then_inc(k_split, 1)

            def split_queries(b, step):
                dve.wait_ge(scratch_emptied, step + 1)
                if later(b):
                    dve.wait_ge(q_stacked, b)
                flat = q_parts[:].rearrange("p g q -> p (g q)")
                nc.vector.tensor_copy(flat, q_full[:]).then_inc(q_hi_ready, 1)
                dve.wait_ge(q_hi_ready, b + 1)
                nc.vector.tensor_tensor(flat[P // 2:P, :], q_full[P // 2:P, :],
                                        flat[P // 2:P, :].bitcast(F32), ALU.subtract
                                        ).then_inc(q_split, 1)

            def split(name, k, b, step):
                if name == "key":
                    split_keys(b, k, step)
                if name == "query":
                    split_queries(b, step)

            def take_values(p, k, step):
                dve.wait_ge(scratch_filled, step + 1)
                nc.vector.tensor_copy(v_ones[p][:, k * KC:(k + 1) * KC, :, 0:2 * DH],
                                      scratch[:].rearrange("p (t n d) -> p t n d", t=KC, n=PAIRS)
                                      ).then_inc(scratch_emptied, 1)

            def first_keys(k):
                cols = KEY_COLS[k]
                dve.wait_ge(keys_projected, k + 1)
                nc.vector.tensor_copy(k_hi[:, cols], scores[:, 1, k, 0:KEYS[k]]).then_inc(k_hi_ready, 1)
                dve.wait_ge(k_hi_ready, k + 1)
                nc.vector.tensor_tensor(k_lo[:, cols], scores[:, 1, k, 0:KEYS[k]], k_hi[:, cols].bitcast(F32),
                                        ALU.subtract).then_inc(k_split, 1)

            def moments_of(r):
                if r < 2:
                    dve.wait_ge(x_loaded[r], 16)
                for b in range(r * QB, (r + 1) * QB):
                    ins = nc.vector.bn_stats(stats[:, b, :], x_all[:, b, :])
                ins.then_inc(stats_ready, 1)
                dve.wait_ge(stats_ready, r + 1)
                for b in range(r * QB, (r + 1) * QB):
                    ins = nc.vector.bn_aggr(moments[:, b, :], stats[:, b, :])
                ins.then_inc(moments_ready, 1)

            def first_norm(r):
                dve.wait_ge(rstd_ready, r + 1)
                for j in range(QB):
                    b = r * QB + j
                    nc.vector.tensor_scalar(normed[r][:, j, :], x_all[:, b, :], moments[:, b, 0:1],
                                            rstd[:, b:b + 1], ALU.subtract, ALU.mult).then_inc(normed_ready, 1)

            dve.wait_ge(mask_loaded, 16)
            nc.vector.tensor_copy(mask_rows[:], mask_u8[:]).then_inc(mask_cast, 1)
            dve.wait_ge(own_head_step, 3)
            nc.vector.tensor_reduce(head_mask[:], own_head[:].rearrange("p t h -> p h t"), AX.X, ALU.add
                                    ).then_inc(head_mask_ready, 1)
            moments_of(0)
            moments_of(1)
            for k in range(KSTEPS):
                first_keys(k)
            for r in range(2):
                first_norm(r)
            for r in range(2, QSTEPS):
                moments_of(r)
                if r == 3:
                    split_queries(0, ALONE.index(("query", 0)))
            for r in range(2, DVE_NORMS):
                first_norm(r)
            dve.wait_ge(mask_in_psum, 1)
            nc.vector.tensor_copy(mask_f[:], scores[0:SQ, 0, 2, 0:B]).then_inc(mask_ready, 1)
            dve.wait_ge(ids_step, 4)
            nc.vector.tensor_copy(expert_ids[:], expert_ids_i[:]).then_inc(ids_step, 1)
            nc.vector.tensor_copy(base[:], base_i[:]).then_inc(ids_step, 1)
            nc.vector.tensor_copy(first_row[:], base_i[0:1, :]).then_inc(ids_step, 1)
            nc.vector.tensor_copy(home[:], home_i[:]).then_inc(homes_next, 1)
            nc.vector.tensor_copy(tile_no[:], tile_i[:]).then_inc(ids_step, 1)
            dve.wait_ge(ids_step, 8)

            def clip(b, c):
                dve.wait_ge(exp_ready, CHUNKS * b + c + 1)
                chunk = probs[:, c % RING, :, :].rearrange("p m q -> p (m q)")
                nc.vector.tensor_scalar(chunk, chunk, LOW, HIGH, ALU.max, ALU.min).then_inc(probs_ready, 1)

            def take_sums(b):
                dve.wait_ge(pv_done, HALVES * (b + 1))
                nc.vector.tensor_copy(o_raw[:], o_sum[:, 0:GQ]).then_inc(o_taken, 1)

            def heads(f, step):
                dve.wait_ge(scratch_filled, step + 1)
                sums = scratch[0:SQ, :].rearrange("q (s h g w) -> q s h g w", s=2, h=2, g=GROUPS)
                nc.vector.reciprocal(rden[:].rearrange("q (s h) g -> q s h g", s=2),
                                     sums[:, :, :, :, 2 * DH]).then_inc(rden_ready, 1)
                dve.wait_ge(rden_ready, f + 1)
                for h in range(2):
                    dst = attn[:].rearrange("q (g s h d) -> q s h g d", g=GROUPS, s=2, h=2)[:, :, h, :, :]
                    r = rden[:].rearrange("q (s h) g -> q s h g", s=2)[:, :, h, :]
                    ins = nc.vector.tensor_tensor(
                        dst, sums[:, :, h, :, h * DH:(h + 1) * DH],
                        r.unsqueeze(3).broadcast_to([SQ, 2, GROUPS, DH]), ALU.mult)
                ins.then_inc(scratch_emptied, 1)

            def tokens_of(f):
                return x_all[:, bass.ds(f, 1), :].rearrange("q o d -> q (o d)")

            def project(f, step):
                dve.wait_ge(scratch_filled, step + 1)
                if isinstance(f, int) and f == 0:
                    dve.wait_ge(mask_ready, 1)
                nc.vector.scalar_tensor_tensor(out=tokens_of(f), in0=scratch[0:SQ, 0:D],
                                               scalar=mask_f[:, bass.ds(f, 1)], in1=tokens_of(f),
                                               op0=ALU.mult, op1=ALU.add).then_inc(scratch_emptied, 1)
                dve.wait_ge(scratch_emptied, step + 1)
                carry_wait(dve, dve_passed)
                nc.vector.bn_stats(stats1[:], tokens_of(f)).then_inc(stats1_ready, 1)
                dve.wait_ge(stats1_ready, f + 1)
                carry_wait(dve, dve_passed)
                nc.vector.bn_aggr(moments1[:], stats1[:]).then_inc(moments1_ready, 1)

            def norm_tokens(f):
                dve.wait_ge(rstd1_ready, f + 1)
                if later(f):
                    dve.wait_ge(rows_sent, 16 * TOP * f)
                for k in range(TOP):
                    ins = nc.vector.tensor_scalar(rows[:, k, TOKEN:D], tokens_of(f), moments1[:, 0:1],
                                                  rstd1[:, 1:2], ALU.subtract, ALU.mult)
                ins.then_inc(rows_ready, 1)

            def best_two(f, step):
                dve.wait_ge(scratch_filled, step + 1)
                nc.vector.tensor_copy(logits[:], scratch[0:SQ, 0:E]).then_inc(scratch_emptied, 1)
                dve.wait_ge(scratch_emptied, step + 1)
                carry_wait(dve, dve_passed)
                nc.vector.max(top8[:], logits[:]).then_inc(top_ready, 1)
                dve.wait_ge(top_ready, f + 1)
                carry_wait(dve, dve_passed)
                nc.vector.max_index(top_at[:], top8[:], logits[:]).then_inc(top_at_ready, 1)
                nc.vector.tensor_tensor(gate_diff[:], top8[:, 1:2], top8[:, 0:1], ALU.subtract
                                        ).then_inc(gate_diff_ready, 1)

            def pick(f):
                dve.wait_ge(top_at_ready, f + 1)
                nc.vector.tensor_copy(top_atf[:], top_at[:, 0:TOP]).then_inc(top_atf_ready, 1)
                dve.wait_ge(top_atf_ready, f + 1)
                nc.vector.tensor_tensor(picks[:], expert_ids[:].unsqueeze(1).broadcast_to([SQ, TOP, E]),
                                        top_atf[:].unsqueeze(2).broadcast_to([SQ, TOP, E]), ALU.is_equal
                                        ).then_inc(picks_ready, 1)
                dve.wait_ge(picks_ready, f + 1)
                nc.vector.tensor_tensor(chosen[:], picks[:, 0, :], picks[:, 1, :], ALU.add).then_inc(chosen_ready, 1)

            def rank(f, step):
                dve.wait_ge(gate_exp_ready, f + 1)
                nc.vector.tensor_scalar(gate_sum[:], gate_exp[:], 1.0, None, ALU.add).then_inc(gate_sum_ready, 1)
                dve.wait_ge(scratch_filled, step + 1)
                nc.vector.tensor_tensor(place[:], scratch[0:SQ, 0:E], base[:], ALU.add).then_inc(place_ready, 1)
                dve.wait_ge(gate_sum_ready, f + 1)
                nc.vector.reciprocal(rows[:, 0, WEIGHT:WEIGHT + 1], gate_sum[:]).then_inc(weight_ready, 1)
                nc.vector.tensor_tensor(base[:], scratch[0:SQ, E:2 * E], base[:], ALU.add
                                        ).then_inc(scratch_emptied, 1)
                dve.wait_ge(place_ready, f + 1)
                nc.vector.tensor_tensor(place_of[:], picks[:], place[:].unsqueeze(1).broadcast_to([SQ, TOP, E]),
                                        ALU.mult).then_inc(place_of_ready, 1)
                dve.wait_ge(weight_ready, f + 1)
                nc.vector.tensor_tensor(rows[:, 1, WEIGHT:WEIGHT + 1], rows[:, 0, WEIGHT:WEIGHT + 1], gate_exp[:],
                                        ALU.mult).then_inc(weights_ready, 1)
                dve.wait_ge(place_of_ready, f + 1)
                nc.vector.tensor_reduce(row_at[:], place_of[:], AX.X, ALU.add).then_inc(row_at_ready, 1)
                dve.wait_ge(row_at_ready, f + 1)
                nc.vector.tensor_copy(row_atu[:], row_at[:]).then_inc(routes_ready, 1)

            def finish(name, f, step):
                if name == "heads":
                    heads(f, step)
                if name == "project":
                    project(f, step)
                if name == "gate":
                    best_two(f, step)
                if name == "rank":
                    rank(f, step)

            def attend(p, b):
                for c in range(CHUNKS):
                    if c == HALF_AT[-1] + 1 - CHUNKS and later(b):
                        take_sums(b - 1)
                    if c >= 1:
                        clip(b, c - 1)
                    elif later(b):
                        clip(b - 1, CHUNKS - 1)
                    name, k = planned(b, c)
                    if later(b) and c == PROJECTED + 2:
                        norm_tokens(b - 1)
                    if name == "value":
                        take_values(1 - p, k, scratch_step(b, c))
                    if c:
                        split(*planned(b, c - 1), b + 1, scratch_step(b, c - 1))
                    finish(name, b - 1, scratch_step(b, c))
                    if later(b) and c == GATED + 1:
                        pick(b - 1)

            attend(0, 0)
            attend(1, 1)
            with dve.Fori(1, B // 2 - 1) as i:
                attend(0, 2 * i)
                attend(1, 2 * i + 1)
            attend(0, B - 2)
            attend(1, B - 1)
            clip(B - 1, CHUNKS - 1)
            take_sums(B - 1)
            for n, (name, k) in enumerate(FINISH):
                finish(name, B - 1, scratch_step(B - 1, CHUNKS) + n)
                if name == "project":
                    norm_tokens(B - 1)
                if name == "gate":
                    pick(B - 1)

            step = 0

            def chain(ins):
                nonlocal step
                step += 1
                ins.then_inc(table_step, 1)
                dve.wait_ge(table_step, step)

            dve.wait_ge(scratch_emptied, scratch_step(B - 1, CHUNKS) + len(FINISH))
            chain(nc.vector.scalar_tensor_tensor(out=tiles_i[:], in0=base[0:1, :], scalar=float(P - 1),
                                                 in1=first_row[:], op0=ALU.add, op1=ALU.subtract))
            chain(nc.vector.tensor_scalar(tiles_s[:], tiles_i[:], int(math.log2(P)), None, ALU.arith_shift_right))
            chain(nc.vector.tensor_copy(tiles_of[:], tiles_s[:]))
            nc.vector.tensor_scalar(unused[:], tiles_of[:], -1.0, float(CAP // P), ALU.mult, ALU.add
                                    ).then_inc(table_step, 1)
            step += 1
            src = tiles_of
            for n, shift in enumerate((1, 2, 4)):
                dst = ends[n % 2]
                nc.vector.tensor_copy(dst[:, 0:shift], src[:, 0:shift]).then_inc(table_step, 1)
                step += 1
                chain(nc.vector.tensor_tensor(dst[:, shift:E], src[:, shift:E], src[:, 0:E - shift], ALU.add))
                src = dst
            chain(nc.vector.tensor_tensor(passed, src[:].unsqueeze(1).broadcast_to([1, NT, E]),
                                          tile_no[:].unsqueeze(2).broadcast_to([1, NT, E]), ALU.is_le))
            chain(nc.vector.tensor_tensor(passed_unused, passed, unused[:].unsqueeze(1).broadcast_to([1, NT, E]),
                                          ALU.mult))
            chain(nc.vector.tensor_reduce(tile_skipped, passed_unused, AX.X, ALU.add))
            chain(nc.vector.tensor_tensor(tile_row, tile_no[:], tile_skipped, ALU.add))
            nc.vector.tensor_scalar(table[:, 1, :], tile_row, float(P), float(E * CAP), ALU.mult, ALU.min
                                    ).then_inc(table_ready, 1)
            chain(nc.vector.tensor_reduce(tile_passed, passed, AX.X, ALU.add))
            nc.vector.tensor_scalar(table[:, 0, :], tile_passed, float(E - 1), None, ALU.min).then_inc(table_ready, 1)
            dve.wait_ge(table_ready, 2)
            dve.wait_ge(w_experts_loaded, 16 * (1 + E))

            def place_w1(t, n):
                expert = dve.value_load(table[0:1, 0, bass.ds(t, 1)], min_val=0, max_val=E - 1)
                if not isinstance(t, int) or t >= 2:
                    dve.wait_ge(hidden_in_psum, t - 1)
                nc.vector.tensor_copy(w1_tile[:, n % 2, :], w1_sb[:, bass.ds(expert, 1), :].rearrange("p o f -> p (o f)")
                                      ).then_inc(w1_ready, 1)

            def take_home(t, n, i):
                dve.wait_ge(tile_loaded[n], 16 * (i + 1))
                if not isinstance(t, int) or t >= NB:
                    dve.wait_ge(y_sent[n], 16 * i)
                nc.vector.tensor_copy(tile_home[n][:], tile_in[n][:, HOME:HOME + 1]).then_inc(home_ready, 1)

            def weigh(t, n):
                dve.wait_ge(y_in_psum, t + 1)
                nc.vector.tensor_scalar(tile_out[n], scores[:, n % 2, 1, 0:D], tile_in[n][:, WEIGHT:WEIGHT + 1],
                                        None, ALU.mult).then_inc(y_ready, 1)

            place_w1(0, 0)

            def tile(t, n, i):
                if not (isinstance(t, int) and t == NT - 1):
                    place_w1(t + 1, n + 1)
                take_home(t, n, i)
                if not (isinstance(t, int) and t == 0):
                    weigh(t - 1, (n - 1) % NB)

            for n in range(NB):
                tile(n, n, 0)
            with dve.Fori(1, NT // NB) as i:
                for n in range(NB):
                    tile(NB * i + n, n, i)
            tile(NT - 1, 0, NT // NB)
            weigh(NT - 1, 0)

            add_outputs(dve, nc.vector, 0, YB - YPOOL, y_step, out_ready)


_INS = ['x', 'ctx_1024', 'mask_BxS_bf1', 'L0_xattn_W_q', 'L0_xattn_W_k', 'L0_xattn_W_v', 'L0_xattn_W_o',
        'L0_ffn_gate_w', 'L0_ffn_w1', 'L0_ffn_w2']
_OUTS = [((32, 100, 128), 'float32')]


def kernel(**inputs):
    import numpy as _np
    import concourse.bacc as _bacc
    from concourse import mybir as _mybir
    from concourse.bass_utils import run_bass_kernel_spmd as _run

    nc = _bacc.Bacc("TRN2", target_bir_lowering=False, num_devices=1)
    arrays, args = {}, []
    for name in _INS:
        a = _np.ascontiguousarray(inputs[name])
        if a.dtype == _np.bool_:
            a = a.view(_np.uint8)
        arrays[f"in_{name}_dram"] = a
        args.append(nc.dram_tensor(f"in_{name}_dram", a.shape, _mybir.dt.from_np(a.dtype), kind="ExternalInput").ap())
    for i, (shape, dtype) in enumerate(_OUTS):
        dt = _mybir.dt.from_np(_np.dtype(dtype))
        args.append(nc.dram_tensor(f"out_{i}_dram", shape, dt, kind="ExternalOutput").ap())
    xattn_moe(nc, *args)
    r = _run(nc, [arrays], core_ids=[0])
    got = tuple(r.results[0][f"out_{i}_dram"] for i in range(len(_OUTS)))
    return got[0]
```
